# Optimizing a Trainium2 kernel written in Bass

```python
import numpy as np
import jax
import jax.numpy as jnp

def _softmax(x, axis=-1):
    return jax.nn.softmax(x, axis=axis)

def _gelu(x):
    return jax.nn.gelu(x, approximate=True)

def _silu(x):
    return jax.nn.silu(x)

def _sigmoid(x):
    return jax.nn.sigmoid(x)

def _layernorm(x, axis=-1, eps=1e-05):
    m = jnp.mean(x, axis=axis, keepdims=True)
    v = jnp.var(x, axis=axis, keepdims=True)
    return (x - m) / jnp.sqrt(v + eps)

def _scatter_add(tgt, idx, src, axis=0):
    return tgt.at[idx].add(src)

def _segment_sum(src, seg, n):
    return jax.ops.segment_sum(src, seg, n)
kernel_name = 'mk_metaformer_d1_conv_nchw256_r2_8085ef'

def setup_inputs(seed: int=0):
    np.random.seed(seed)
    _w = jnp.asarray

    def _rec_inputs():
        import jax
        import jax.numpy as jnp
        _gk = jax.random.key(seed)
        x = -0.0005153 + 1.001 * jax.random.normal(jax.random.fold_in(_gk, 1), (4, 128, 56, 56), jnp.float32)
        return x
    x = _rec_inputs()

    def _L0_conv_setup():
        import jax, jax.numpy as jnp
        import numpy as np
        B, C, G, K, S, P, R = (4, 128, 16, 7, 1, 3, 4)
        H = W = 56
        key = jax.random.key(seed)
        k1, k2, k3 = jax.random.split(key, 3)
        x = jax.random.normal(k1, (B, C, H, W), jnp.float32)
        reduce_w = jax.random.normal(k2, (C // R, C), jnp.float32) * 0.05
        reduce_b = jnp.zeros((C // R,), jnp.float32)
        span_w = jax.random.normal(k3, (K * K * G, C // R), jnp.float32) * 0.05
        span_b = jnp.zeros((K * K * G,), jnp.float32)
        return {'x': x, 'reduce_w': reduce_w, 'reduce_b': reduce_b, 'span_w': span_w, 'span_b': span_b}
    _L0_conv_all = _L0_conv_setup()
    _L0_conv_in = {k: v for k, v in _L0_conv_all.items() if k in ('reduce_w', 'reduce_b', 'span_w', 'span_b')}
    del _L0_conv_all

    def _L0_ffn_setup():
        import jax, jax.numpy as jnp
        import numpy as np
        N_EXPERTS = 8
        TOP_K = 2
        key = jax.random.key(seed)
        ks = jax.random.split(key, 5)
        B, T, C, E, H = (8, 1024, 128, 8, 341)
        scale = 1.0 / np.sqrt(C)
        return {'x': jax.random.normal(ks[0], (B, T, C), dtype=jnp.float32), 'router_w': jax.random.normal(ks[1], (E, C), dtype=jnp.float32) * scale, 'w1': jax.random.normal(ks[2], (E, H, C), dtype=jnp.float32) * scale, 'w2': jax.random.normal(ks[3], (E, C, H), dtype=jnp.float32) * (1.0 / np.sqrt(H)), 'w3': jax.random.normal(ks[4], (E, H, C), dtype=jnp.float32) * scale}
    _L0_ffn_all = _L0_ffn_setup()
    _L0_ffn_in = {k: v for k, v in _L0_ffn_all.items() if k in ('router_w', 'w1', 'w2', 'w3')}
    del _L0_ffn_all
    return {'x': x, 'L0_conv_reduce_w': _L0_conv_in['reduce_w'], 'L0_conv_reduce_b': _L0_conv_in['reduce_b'], 'L0_conv_span_w': _L0_conv_in['span_w'], 'L0_conv_span_b': _L0_conv_in['span_b'], 'L0_ffn_router_w': _L0_ffn_in['router_w'], 'L0_ffn_w1': _L0_ffn_in['w1'], 'L0_ffn_w2': _L0_ffn_in['w2'], 'L0_ffn_w3': _L0_ffn_in['w3']}

def reference(x, L0_conv_reduce_w, L0_conv_reduce_b, L0_conv_span_w, L0_conv_span_b, L0_ffn_router_w, L0_ffn_w1, L0_ffn_w2, L0_ffn_w3):
    import jax
    import jax.numpy as jnp

    def _L0_conv_ref(x, reduce_w, reduce_b, span_w, span_b):
        import jax, jax.numpy as jnp
        import numpy as np
        B, C, G, K, S, P, R = (4, 128, 16, 7, 1, 3, 4)
        H = W = 56
        b, c, h_in, w_in = x.shape
        Ho = (h_in + 2 * P - K) // S + 1
        Wo = (w_in + 2 * P - K) // S + 1
        patches = jax.lax.conv_general_dilated_patches(x, (K, K), (S, S), [(P, P), (P, P)])
        patches = patches.reshape(b, G, c // G, K * K, Ho, Wo)
        if S > 1:
            xk = jax.lax.reduce_window(x, 0.0, jax.lax.add, (1, 1, S, S), (1, 1, S, S), 'VALID') / (S * S)
        else:
            xk = x
        h = jnp.einsum('bchw,oc->bohw', xk, reduce_w) + reduce_b[None, :, None, None]
        kern = jnp.einsum('bchw,oc->bohw', h, span_w) + span_b[None, :, None, None]
        kern = kern.reshape(b, G, 1, K * K, Ho, Wo)
        out = (kern * patches).sum(axis=3)
        return out.reshape(b, c, Ho, Wo)

    def _L0_ffn_ref(x, router_w, w1, w2, w3):
        import jax, jax.numpy as jnp
        import numpy as np
        N_EXPERTS = 8
        TOP_K = 2
        B, T, C = x.shape
        flat = x.reshape(-1, C)
        logits = flat @ router_w.T
        probs = jax.nn.softmax(logits, axis=-1)
        topk_probs, topk_idx = jax.lax.top_k(probs, TOP_K)
        topk_probs = topk_probs / (jnp.sum(topk_probs, axis=-1, keepdims=True) + 1e-09)
        onehot = jax.nn.one_hot(topk_idx, N_EXPERTS, dtype=flat.dtype)
        gates = jnp.einsum('nk,nke->ne', topk_probs, onehot)
        h1 = jnp.einsum('nc,ehc->neh', flat, w1)
        h3 = jnp.einsum('nc,ehc->neh', flat, w3)
        h = jax.nn.silu(h1) * h3
        y = jnp.einsum('neh,ech->nec', h, w2)
        out = jnp.einsum('ne,nec->nc', gates, y)
        return out.reshape(B, T, C)

    def _gn(v, G=32, eps=1e-05):
        B_, C_, H_, W_ = v.shape
        g = v.reshape(B_, G, C_ // G, H_, W_)
        m = jnp.mean(g, axis=(2, 3, 4), keepdims=True)
        s = jnp.var(g, axis=(2, 3, 4), keepdims=True)
        return ((g - m) / jnp.sqrt(s + eps)).reshape(v.shape)

    def _ln_c(v, eps=1e-06):
        m = jnp.mean(v, axis=1, keepdims=True)
        s = jnp.var(v, axis=1, keepdims=True)
        return (v - m) / jnp.sqrt(s + eps)

    def _ln_t(v, eps=1e-05):
        m = jnp.mean(v, axis=-1, keepdims=True)
        s = jnp.var(v, axis=-1, keepdims=True)
        return (v - m) / jnp.sqrt(s + eps)

    def _to_tokens(v):
        B_, C_, H_, W_ = v.shape
        return v.reshape(B_, C_, H_ * W_).transpose(0, 2, 1)

    def _from_tokens(t, like):
        B_, C_, H_, W_ = like.shape
        return t.transpose(0, 2, 1).reshape(B_, C_, H_, W_)
    x = x + _L0_conv_ref(_ln_c(x), L0_conv_reduce_w, L0_conv_reduce_b, L0_conv_span_w, L0_conv_span_b)
    t = _to_tokens(x)
    t = t + _L0_ffn_ref(_ln_t(t), L0_ffn_router_w, L0_ffn_w1, L0_ffn_w2, L0_ffn_w3)
    x = _from_tokens(t, x)
    return x

_drawn_inputs = setup_inputs


def setup_inputs(seed=0):
    import zlib

    import numpy as np

    out = dict(_drawn_inputs(seed))
    spreads = {'L0_conv_reduce_b': (0.0, 0.1), 'L0_conv_span_b': (0.0, 0.1)}
    factors = {}
    for name, (base, spread) in spreads.items():
        noise = np.random.default_rng([zlib.crc32(name.encode()), seed]).standard_normal(out[name].shape)
        drawn = base * np.exp(spread * noise) if base else spread * noise
        out[name] = jnp.asarray(drawn.astype(out[name].dtype))
    for name, factor in factors.items():
        out[name] = (out[name] * factor).astype(out[name].dtype)
    return out
```

```python
from contextlib import ExitStack

import concourse.bass as bass
from concourse import mybir

F32 = mybir.dt.float32
F32R = mybir.dt.float32r
U32 = mybir.dt.uint32
ALU = mybir.AluOpType
ACT = mybir.ActivationFunctionType
AX = mybir.AxisListType.X

B, C, H, W = 4, 128, 56, 56
GROUPS, KS, PAD, RED = 16, 7, 3, 32
EXPERTS, HID = 8, 341
LN_C_EPS, LN_T_EPS, GATE_EPS = 1e-6, 1e-5, 1e-9

ROWS = 8
N = ROWS * W
SUBS, SUB = 4, N // 4
PER_IMG = H // ROWS
TILES = B * PER_IMG
PW = W + 2 * PAD
IMG = (H + 2 * PAD) * PW

CPE = 3
HC = -(-HID // CPE)
CH = EXPERTS * CPE

PAIRS = [(dy * PW + dx, 1) for dy in range(KS) for dx in (0, 2, 4)] + [(dy * PW + 6, PW) for dy in (0, 2, 4)]
SINGLE = 6 * PW + 6
TAPS = len(PAIRS) + 1
TAP_ORDER = [(dy * KS + dx + i) for dy in range(KS) for dx in (0, 2, 4) for i in (0, 1)] + [
    (dy + i) * KS + 6 for dy in (0, 2, 4) for i in (0, 1)] + [KS * KS - 1]

BY_VECTOR = (5, 10, 15, 20)
BY_POOL = [u for u in range(2, TAPS - 1) if u not in BY_VECTOR]
POOL_OPS = len(BY_POOL) + 1
PRING = 3

GW = 72

STEPS = CH
UNITS_AT = {s: [] for s in range(STEPS)}
_u = 0
for _s in range(1, STEPS):
    for _ in range(2 if _s in (9, 17) else 1):
        UNITS_AT[_s].append(_u)
        _u += 1
assert _u == TAPS
LAG = 2

BANK_AT = {s: [] for s in range(STEPS)}
BANK_AT[0].append(("conv", "h"))
BANK_AT[3].append(("ln2", "x1_t"))
BANK_AT[4].append(("ln1", "x_t"))
BANK_AT[10].append(("ln2", "xn2"))
BANK_AT[12].append(("ln2", "logits"))
BANK_AT[12].append(("ln1", "xn"))
for _e in range(EXPERTS):
    BANK_AT[CPE * _e + 2].append(("ffn", f"gate{_e}"))
BANK_AT[23].append(("ln2", "gates_t"))

AHEAD = {"ln1": 4, "conv": 2, "ln2": 1, "ffn": 0, "tail": -1}


def bodies():
    out = []
    for t in range(-4, TILES + 1):
        stages = tuple(s for s, a in AHEAD.items() if 0 <= t + a < TILES)
        first = t == 0 or t + AHEAD["conv"] == 0 or t + AHEAD["ln2"] == 0 or t + AHEAD["ln1"] == 0
        if out and out[-1][2] == stages and not out[-1][3] and not first:
            out[-1][1] = t + 1
        else:
            out.append([t, t + 1, stages, first])
    return [(a, b, s) for a, b, s, _ in out]


def bank_uses(stages):
    return [name for s in range(STEPS) for stage, name in BANK_AT[s] if stage in stages]


def build(nc, x, w_red, b_red, w_span, router, w1, w3, w2, ident, select, iota, out):
    with ExitStack() as ctx:
        def sb(name, shape, dt=F32):
            return ctx.enter_context(nc.sbuf_tensor(name, shape, dt))

        def psum(name, shape):
            return ctx.enter_context(nc.psum_tensor(name, shape, F32))

        def sem(name):
            return ctx.enter_context(nc.semaphore(name))

        kern_ps = psum("kern_ps", [C, 2, 2, 512])
        h1_ps = psum("h1_ps", [C, 512])
        h3_ps = psum("h3_ps", [C, 512])
        y_ps = psum("y_ps", [C, 512])
        bank = psum("bank", [C, 512])

        w1_hi, w1_lo = sb("w1_hi", [C, CH * HC], F32R), sb("w1_lo", [C, CH * HC], F32R)
        w3_hi, w3_lo = sb("w3_hi", [C, CH * HC], F32R), sb("w3_lo", [C, CH * HC], F32R)
        w2_sb = sb("w2_sb", [HC, CH, C])
        span = sb("span", [98, KS * KS * C], F32R)
        red_sb = sb("red_sb", [C, 3 * RED])
        bred_sb = sb("bred_sb", [3 * RED, 1])
        router_sb = sb("router_sb", [C, EXPERTS])
        ident_sb = sb("ident_sb", [C, C])
        select_raw = sb("select_raw", [40, EXPERTS * C])
        select_sb = sb("select_sb", [40, EXPERTS * C], F32R)
        iota_sb = sb("iota_sb", [SUB, SUBS, EXPERTS])
        minus_half = sb("minus_half", [SUB, SUBS])
        euler = sb("euler", [SUB, SUBS * EXPERTS])

        xn = sb("xn", [C, 2 * IMG])
        x_ln = sb("x_ln", [C, N])
        x_res = sb("x_res", [C, N])
        h_stack = sb("h_stack", [98, N], F32R)
        h_full = sb("h_full", [2 * RED, N])
        prod = sb("prod", [C, PRING, 2 * N])
        prod_v = sb("prod_v", [C, 2 * N])
        acc_p = sb("acc_p", [C, 2 * N])
        acc_v = sb("acc_v", [C, 2 * N])
        single = sb("single", [C, N])

        tok = {k: sb(f"tok_{k}", [SUB, SUBS, C]) for k in ("ln1", "ln2")}
        stats = {k: sb(f"stats_{k}", [SUB, SUBS, 6]) for k in ("ln1", "ln2")}
        mv = {k: sb(f"mv_{k}", [SUB, SUBS, 2]) for k in ("ln1", "ln2")}
        veps = {k: sb(f"veps_{k}", [SUB, SUBS]) for k in ("ln1", "ln2")}
        rstd = {k: sb(f"rstd_{k}", [SUB, SUBS]) for k in ("ln1", "ln2")}
        shift = {k: sb(f"shift_{k}", [SUB, SUBS]) for k in ("ln1", "ln2")}
        logits = sb("logits", [SUB, SUBS, EXPERTS])
        lmax = sb("lmax", [SUB, SUBS])
        ldiff = sb("ldiff", [SUB, SUBS, EXPERTS])
        lexp = sb("lexp", [SUB, SUBS, EXPERTS])
        lsum = sb("lsum", [SUB, SUBS])
        rsum = sb("rsum", [SUB, SUBS])
        probs = sb("probs", [SUB, SUBS, EXPERTS])
        top = sb("top", [SUB, SUBS, EXPERTS])
        top_at = sb("top_at", [SUB, SUBS, EXPERTS], U32)
        top_atf = sb("top_atf", [SUB, SUBS, 2])
        gden = sb("gden", [SUB, SUBS])
        grec = sb("grec", [SUB, SUBS])
        gtop = sb("gtop", [SUB, SUBS, 2])
        hot0 = sb("hot0", [SUB, SUBS, EXPERTS])
        hot1 = sb("hot1", [SUB, SUBS, EXPERTS])
        gates = sb("gates", [SUB, SUBS, GW])
        gate_t = sb("gate_t", [40, N], F32R)
        gate_f = sb("gate_f", [40, N])

        nothing = sb("nothing", [1, 1])

        x1 = sb("x1", [C, N])
        x1_res = sb("x1_res", [C, N])
        xn2 = sb("xn2", [C, N])
        xf_hi, xf_lo = sb("xf_hi", [C, N], F32R), sb("xf_lo", [C, N], F32R)
        silu = sb("silu", [HC, 2, N])
        hid = sb("hid", [HC, 3, N])
        gate_b = sb("gate_b", [C, 2, N])
        gy = sb("gy", [C, 2, N])
        y_acc = sb("y_acc", [C, N])
        y_out = sb("y_out", [C, N])

        s_const = sem("s_const")
        s_stage = [sem(f"s_stage{i}") for i in range(PRING)]
        s_piece_hi = sem("s_piece_hi")
        s_piece_lo = sem("s_piece_lo")
        s_piece_b = sem("s_piece_b")
        s_set = sem("s_set")
        s_setp = sem("s_setp")
        s_sel = sem("s_sel")
        s_bank = sem("s_bank")
        s_bank_out = sem("s_bank_out")
        s_x_ln = sem("s_x_ln")
        s_x_res = sem("s_x_res")
        s_ln = {k: sem(f"s_{k}_v") for k in ("ln1", "ln2")}
        s_rstd = {k: sem(f"s_{k}_rstd") for k in ("ln1", "ln2")}
        s_tok = {k: sem(f"s_{k}_tok") for k in ("ln1", "ln2")}
        s_h_lo = sem("s_h_lo")
        s_kern = sem("s_kern")
        s_prod = sem("s_prod")
        s_accv = sem("s_accv")
        s_accp = sem("s_accp")
        s_x1 = sem("s_x1")
        s_x1_res = sem("s_x1_res")
        s_rt = sem("s_rt")
        s_exp = sem("s_exp")
        s_gate_lo = sem("s_gate_lo")
        s_xf_hi = sem("s_xf_hi")
        s_xf_lo = sem("s_xf_lo")
        s_h1 = sem("s_h1")
        s_silu = sem("s_silu")
        s_h3 = sem("s_h3")
        s_hid = sem("s_hid")
        s_w2 = sem("s_w2")
        s_gy = sem("s_gy")
        s_y = sem("s_y")
        s_out = sem("s_out")

        RT = 17
        NCONST = 8

        span_pieces = [("span", i) for i in range(KS)]
        w_pieces = [(w, i) for w in ("w1", "w3") for i in range(4)]
        PIECES = span_pieces + w_pieces
        WCOLS = CH * HC // 4
        SCOLS = KS * C

        def after(eng, s, per, tile, k):
            v = tile * per + k
            if not isinstance(v, int) or v > 0:
                eng.wait_ge(s, v)

        def after_apart(s, per, tile, k):
            after(nc.vector, s, per, tile, k)
            nc.vector.memset(nothing[:], 0.0)

        def run(eng, body):
            base = 0
            for first, end, stages in bodies():
                uses = len(bank_uses(stages))
                if end - first == 1:
                    body(first, stages, base)
                else:
                    with eng.Fori(first, end) as t:
                        body(t, stages, (t - first) * uses + base)
                base += uses * (end - first)

        def bank_count(stages, base, name):
            return base + bank_uses(stages).index(name) + 1

        def xn_at(tile):
            return ((tile // PER_IMG) % 2) * IMG + (tile % PER_IMG) * (ROWS * PW)

        def window(start, pair_step=None):
            pdim = list(xn[:, 0:1].ap[0])
            dims = ([[pair_step, 2]] if pair_step else []) + [[PW, ROWS], [1, W]]
            return bass.AP(tensor=xn[:, 0:1].tensor, offset=start, ap=[pdim] + dims)

        def rows(ap):
            return ap.rearrange("p (r w) -> p r w", w=W)

        def pair_rows(ap):
            return ap.rearrange("p (i r w) -> p i r w", i=2, w=W)

        block = ctx.enter_context(nc.Block())

        @block.sync
        def _(sp):
            for dst, src in ((ident_sb[:], ident), (red_sb[:], w_red), (bred_sb[:], b_red), (router_sb[:], router),
                             (select_raw[:], select), (iota_sb[:].rearrange("p a b -> p (a b)"), iota)):
                sp.dma_start(dst, src).then_inc(s_const, 16)
            for i, (kind, k) in enumerate(PIECES):
                if i >= PRING:
                    sp.wait_ge(s_piece_lo, i - PRING + 1)
                if i - PRING in range(len(span_pieces)):
                    sp.wait_ge(s_piece_b, i - PRING + 1)
                if kind == "span":
                    sp.dma_start(prod[0:98, i % PRING, 0:SCOLS], w_span[:, k * SCOLS:(k + 1) * SCOLS]).then_inc(s_stage[i % PRING], 16)
                else:
                    src = (w1 if kind == "w1" else w3)[:, k * WCOLS:(k + 1) * WCOLS]
                    sp.dma_start(prod[:, i % PRING, 0:WCOLS], src).then_inc(s_stage[i % PRING], 16)
            sp.dma_start(w2_sb[:].rearrange("p a b -> p (a b)"), w2).then_inc(s_const, 16)

            def body(t, stages, base):
                if "ln1" in stages:
                    after(sp, s_tok["ln1"], 1, t + AHEAD["ln1"], 0)
                    sp.dma_start(x_ln[:], x[:, bass.ds((t + AHEAD["ln1"]) * N, N)]).then_inc(s_x_ln, 16)
                if "conv" in stages:
                    after(sp, s_accp, POOL_OPS, t + AHEAD["conv"], 0)
                    sp.dma_start(x_res[:], x[:, bass.ds((t + AHEAD["conv"]) * N, N)]).then_inc(s_x_res, 16)
                if "tail" in stages:
                    after(sp, s_y, EXPERTS, t - 1, EXPERTS)
                    sp.dma_start(out[:, bass.ds((t - 1) * N, N)], y_out[:]).then_inc(s_out, 16)

            run(sp, body)
            sp.wait_ge(s_out, 16 * TILES)

        @block.tensor
        def _(pe):
            mm = nc.tensor.matmul

            def body(t, stages, base):
                f, c = t, t + AHEAD["conv"]
                used = [0]

                def take_bank():
                    v = base + used[0]
                    if not isinstance(v, int) or v > 0:
                        pe.wait_ge(s_bank_out, v)
                    used[0] += 1

                def bank_use(stage, name):
                    take_bank()
                    if name == "h":
                        i = mm(bank[0:3 * RED, 0:N], red_sb[:], window(xn_at(c) + PAD * PW + PAD), start=True, stop=True)
                    elif name in ("x_t", "x1_t"):
                        if name == "x_t":
                            after(pe, s_x_ln, 16, t + AHEAD["ln1"], 16)
                        else:
                            after(pe, s_x1, 3, t + AHEAD["ln2"], 3)
                        src = x_ln if name == "x_t" else x1
                        for k in range(SUBS):
                            i = nc.tensor.transpose(bank[0:SUB, k * C:(k + 1) * C], src[:, k * SUB:(k + 1) * SUB], ident_sb[:])
                    elif name in ("xn", "xn2"):
                        after(pe, s_tok[stage], 1, t + AHEAD[stage], 1)
                        for k in range(SUBS):
                            i = nc.tensor.transpose(bank[:, k * SUB:(k + 1) * SUB], tok[stage][:, k, :], ident_sb[0:SUB, 0:SUB])
                    elif name == "logits":
                        for k in range(SUBS):
                            i = mm(bank[0:SUB, k * EXPERTS:(k + 1) * EXPERTS], xn2[:, k * SUB:(k + 1) * SUB], router_sb[:],
                                   start=True, stop=True)
                    elif name == "gates_t":
                        after(pe, s_rt, RT, t + AHEAD["ln2"], RT)
                        for k in range(SUBS):
                            i = nc.tensor.transpose(bank[0:GW, k * SUB:(k + 1) * SUB], gates[:, k, :], ident_sb[0:SUB, 0:SUB])
                    else:
                        e = int(name[4:])
                        if e == 0:
                            after(pe, s_gate_lo, 1, f, 1)
                        i = mm(bank[:, 0:N], select_sb[:, e * C:(e + 1) * C], gate_t[:], start=True, stop=True)
                    i.then_inc(s_bank, 1)

                def unit(u):
                    if u == 0:
                        after(pe, s_h_lo, 1, c, 1)
                        after(pe, s_prod, TAPS, c, 0)
                    elif u >= 2:
                        after(pe, s_prod, TAPS, c, u - 1)
                    for i in range(2 if u < TAPS - 1 else 1):
                        k = 2 * u + i
                        last = mm(kern_ps[:, u % 2, i, 0:N], span[:, k * C:(k + 1) * C], h_stack[:], start=True, stop=True)
                    last.then_inc(s_kern, 1)

                def hidden(j, ps, hi, lo, done):
                    a, b = j * HC, (j + 1) * HC
                    mm(ps[0:HC, 0:N], hi[:, a:b], xf_hi[:], start=True, stop=False)
                    mm(ps[0:HC, 0:N], hi[:, a:b], xf_lo[:], start=False, stop=False)
                    mm(ps[0:HC, 0:N], lo[:, a:b], xf_hi[:], start=False, stop=True).then_inc(done, 1)

                def down(tile, j):
                    after(pe, s_hid, CH, tile, j + 1)
                    if j % CPE == 0:
                        after(pe, s_gy, EXPERTS, tile, j // CPE)
                    mm(y_ps[:, 0:N], w2_sb[:, j, :], hid[:, j % 3, :], start=j % CPE == 0,
                       stop=j % CPE == CPE - 1).then_inc(s_w2, 1)

                for j in range(STEPS):
                    if j < LAG:
                        if "tail" in stages:
                            down(f - 1, CH - LAG + j)
                    elif "ffn" in stages:
                        down(f, j - LAG)
                    if j == 0 and "conv" in stages:
                        bank_use("conv", "h")
                    if "ffn" in stages:
                        if j == 0:
                            after(pe, s_xf_lo, 1, f, 1)
                        after(pe, s_silu, CH, f, j)
                        hidden(j, h1_ps, w1_hi, w1_lo, s_h1)
                    if "conv" in stages:
                        for u in UNITS_AT[j]:
                            unit(u)
                    if "ffn" in stages:
                        after(pe, s_hid, CH, f, j)
                        hidden(j, h3_ps, w3_hi, w3_lo, s_h3)
                    for stage, name in BANK_AT[j]:
                        if stage in stages and name != "h":
                            bank_use(stage, name)

            pe.wait_ge(s_const, 16 * 7)
            pe.wait_ge(s_sel, 1)
            pe.wait_ge(s_set, 2)
            pe.wait_ge(s_setp, 2)
            pe.wait_ge(s_piece_lo, len(PIECES))
            pe.wait_ge(s_piece_b, len(span_pieces))
            run(pe, body)

        @block.scalar
        def _(act):
            act_f = nc.scalar.activation

            for i, (kind, k) in enumerate(PIECES):
                act.wait_ge(s_stage[i % PRING], 16 * (i // PRING + 1))
                if kind == "span":
                    dst = span[:, k * SCOLS:(k + 1) * SCOLS]
                    act_f(dst, prod[0:98, i % PRING, 0:SCOLS], ACT.Copy).then_inc(s_piece_hi, 1)
                    act.wait_ge(s_piece_lo, i + 1)
                    act_f(span[96:97, k * SCOLS:(k + 1) * SCOLS], prod[96:97, i % PRING, 0:SCOLS],
                          ACT.Copy).then_inc(s_piece_b, 1)
                else:
                    dst = (w1_hi if kind == "w1" else w3_hi)[:, k * WCOLS:(k + 1) * WCOLS]
                    act_f(dst, prod[:, i % PRING, 0:WCOLS], ACT.Copy).then_inc(s_piece_hi, 1)
            act.wait_ge(s_const, 16 * 7)
            act_f(select_sb[:], select_raw[:], ACT.Copy).then_inc(s_sel, 1)
            act.wait_ge(s_setp, 2)

            def body(t, stages, base):
                f, c = t, t + AHEAD["conv"]
                used = [0]

                def bank_use(stage, name):
                    used[0] += 1
                    act.wait_ge(s_bank, base + used[0])
                    if name == "h":
                        act_f(h_full[RED:2 * RED, :], bank[RED:2 * RED, 0:N], ACT.Identity, bias=bred_sb[RED:2 * RED, 0:1])
                        i = act_f(h_stack[0:3 * RED, :], bank[0:3 * RED, 0:N], ACT.Identity, bias=bred_sb[:, 0:1])
                    elif name in ("x_t", "x1_t"):
                        i = act_f(tok[stage][:], bank[0:SUB, :].rearrange("p (a b) -> p a b", a=SUBS), ACT.Copy)
                    elif name == "xn":
                        dst = window(xn_at(t + AHEAD["ln1"]) + PAD * PW + PAD)
                        i = act_f(dst, rows(bank[:, 0:N]), ACT.Copy)
                    elif name == "xn2":
                        after(act, s_xf_lo, 1, t + AHEAD["ln2"], 0)
                        i = act_f(xn2[:], bank[:, 0:N], ACT.Copy)
                    elif name == "logits":
                        i = act_f(logits[:], bank[0:SUB, 0:SUBS * EXPERTS].rearrange("p (a b) -> p a b", a=SUBS), ACT.Copy)
                    elif name == "gates_t":
                        act_f(gate_f[:], bank[0:40, 0:N], ACT.Copy)
                        i = act_f(gate_t[:], bank[0:40, 0:N], ACT.Copy)
                    else:
                        e = int(name[4:])
                        after(act, s_gy, EXPERTS, f, e - 1)
                        i = act_f(gate_b[:, e % 2, :], bank[:, 0:N], ACT.Copy)
                    i.then_inc(s_bank_out, 1)

                def normalise(stage, tile):
                    after(act, s_ln[stage], 4, tile, 4)
                    for k in range(SUBS):
                        i = act_f(tok[stage][:, k, :], tok[stage][:, k, :], ACT.Identity,
                                  bias=shift[stage][:, k:k + 1], scale=rstd[stage][:, k:k + 1])
                    i.then_inc(s_tok[stage], 1)

                for j in range(STEPS):
                    if j == 0 and "ffn" in stages:
                        after(act, s_h3, CH, f, 0)
                        act_f(xf_hi[:], xn2[:], ACT.Copy).then_inc(s_xf_hi, 1)
                    if j == 0 and "conv" in stages:
                        bank_use("conv", "h")
                    if "ffn" in stages:
                        after(act, s_h1, CH, f, j + 1)
                        after(act, s_hid, CH, f, j - 1)
                        act_f(silu[:, j % 2, :], h1_ps[0:HC, 0:N], ACT.Silu).then_inc(s_silu, 1)
                    for stage, name in BANK_AT[j]:
                        if stage in stages and name != "h":
                            bank_use(stage, name)
                    if j == 8 and "ln2" in stages:
                        normalise("ln2", t + AHEAD["ln2"])
                    if j == 9 and "ln1" in stages:
                        normalise("ln1", t + AHEAD["ln1"])
                    if j == STEPS - 1 and "ln2" in stages:
                        after(act, s_y, EXPERTS, t, 1)
                        act_f(x1_res[:], x1[:], ACT.Copy).then_inc(s_x1_res, 1)

            run(act, body)

        @block.vector
        def _(dve):
            v = nc.vector
            v.memset(h_stack[96:98, :].bitcast(F32), 1.0).then_inc(s_set, 1)
            v.memset(gates[:], 0.0).then_inc(s_set, 1)
            for i, (kind, k) in enumerate(PIECES):
                dve.wait_ge(s_stage[i % PRING], 16 * (i // PRING + 1))
                dve.wait_ge(s_piece_hi, i + 1)
                if kind == "span":
                    hi = span[64:98, k * SCOLS:(k + 1) * SCOLS]
                    v.tensor_tensor(hi, prod[64:98, i % PRING, 0:SCOLS], hi.bitcast(F32), ALU.subtract).then_inc(s_piece_lo, 1)
                else:
                    hi, lo = (w1_hi, w1_lo) if kind == "w1" else (w3_hi, w3_lo)
                    v.tensor_tensor(lo[:, k * WCOLS:(k + 1) * WCOLS], prod[:, i % PRING, 0:WCOLS],
                                    hi[:, k * WCOLS:(k + 1) * WCOLS].bitcast(F32), ALU.subtract).then_inc(s_piece_lo, 1)
            dve.wait_ge(s_piece_b, len(span_pieces))
            dve.wait_ge(s_const, 16 * 7)
            dve.wait_ge(s_set, 2)
            dve.wait_ge(s_setp, 2)

            def body(t, stages, base):
                f, c, l = t, t + AHEAD["conv"], t + AHEAD["ln2"]

                def ln(stage, k, name, eps):
                    tile = t + AHEAD[stage]
                    if k == 0:
                        dve.wait_ge(s_bank_out, bank_count(stages, base, name))
                        for q in range(SUBS):
                            i = v.bn_stats(stats[stage][:, q, :], tok[stage][:, q, :])
                    elif k == 1:
                        after_apart(s_ln[stage], 4, tile, 1)
                        for q in range(SUBS):
                            i = v.bn_aggr(mv[stage][:, q, :], stats[stage][:, q, :])
                    elif k == 2:
                        after(dve, s_ln[stage], 4, tile, 2)
                        i = v.tensor_scalar(veps[stage][:], mv[stage][:, :, 1], eps, None, ALU.add)
                    else:
                        after(dve, s_rstd[stage], 1, tile, 1)
                        i = v.scalar_tensor_tensor(out=shift[stage][:], in0=mv[stage][:, :, 0], scalar=-1.0,
                                                   in1=rstd[stage][:], op0=ALU.mult, op1=ALU.mult)
                    i.then_inc(s_ln[stage], 1)

                def router_step(k):
                    if k == 0:
                        dve.wait_ge(s_bank_out, bank_count(stages, base, "logits"))
                        i = v.tensor_reduce(lmax[:], logits[:], AX, ALU.max)
                    elif k == 2:
                        after(dve, s_exp, 1, l, 1)
                        i = v.tensor_reduce(lsum[:], lexp[:], AX, ALU.add)
                    else:
                        if k in (5, 6):
                            after_apart(s_rt, RT, l, k)
                        else:
                            after(dve, s_rt, RT, l, k)
                    if k == 1:
                        i = v.tensor_tensor(ldiff[:], logits[:], lmax[:].unsqueeze(2).broadcast_to([SUB, SUBS, EXPERTS]), ALU.subtract)
                    elif k == 3:
                        i = v.reciprocal(rsum[:], lsum[:])
                    elif k == 4:
                        i = v.tensor_tensor(probs[:], lexp[:], rsum[:].unsqueeze(2).broadcast_to([SUB, SUBS, EXPERTS]), ALU.mult)
                    elif k == 5:
                        for q in range(SUBS):
                            i = v.max(top[:, q, :], probs[:, q, :])
                    elif k == 6:
                        for q in range(SUBS):
                            i = v.max_index(top_at[:, q, :], top[:, q, :], probs[:, q, :])
                    elif k == 7:
                        i = v.tensor_copy(top_atf[:], top_at[:, :, 0:2])
                    elif k == 8:
                        i = v.tensor_tensor(gden[:], top[:, :, 0], top[:, :, 1], ALU.add)
                    elif k == 9:
                        i = v.tensor_scalar(gden[:], gden[:], GATE_EPS, None, ALU.add)
                    elif k == 10:
                        i = v.reciprocal(grec[:], gden[:])
                    elif k == 11:
                        i = v.tensor_tensor(gtop[:], top[:, :, 0:2], grec[:].unsqueeze(2).broadcast_to([SUB, SUBS, 2]), ALU.mult)
                    elif k in (12, 13):
                        i = v.tensor_tensor((hot0, hot1)[k - 12][:], iota_sb[:],
                                            top_atf[:, :, k - 12:k - 11].broadcast_to([SUB, SUBS, EXPERTS]), ALU.is_equal)
                    elif k in (14, 15):
                        hot = (hot0, hot1)[k - 14]
                        i = v.tensor_tensor(hot[:], hot[:], gtop[:, :, k - 14:k - 13].broadcast_to([SUB, SUBS, EXPERTS]), ALU.mult)
                    elif k == 16:
                        v.tensor_tensor(gates[:, :, 0:EXPERTS], hot0[:], hot1[:], ALU.add)
                        i = v.tensor_tensor(gates[:, :, 32:32 + EXPERTS], hot0[:], hot1[:], ALU.add)
                    i.then_inc(s_rt, 1)

                def unit(u):
                    after(dve, s_kern, TAPS, c, u + 1)
                    start = xn_at(c)
                    if u == TAPS - 1:
                        g = POOL_OPS - 1
                        after(dve, s_accp, POOL_OPS, c, g - PRING + 1)
                        v.tensor_tensor(rows(prod[:, g % PRING, 0:N]), rows(kern_ps[:, u % 2, 0, 0:N]),
                                        window(start + SINGLE), ALU.mult).then_inc(s_prod, 1)
                        return
                    if u == 0:
                        dst = acc_p[:]
                    elif u == 1:
                        dst = acc_v[:]
                    elif u in BY_VECTOR:
                        dst = prod_v[:]
                        after(dve, s_accv, len(BY_VECTOR), c, BY_VECTOR.index(u))
                    else:
                        g = BY_POOL.index(u)
                        after(dve, s_accp, POOL_OPS, c, max(g - PRING + 1, 0))
                        dst = prod[:, g % PRING, :]
                    if u == 0:
                        after(dve, s_x1, 3, c, 0)
                    v.tensor_tensor(pair_rows(dst), kern_ps[:, u % 2, :, 0:N].rearrange("p i (r w) -> p i r w", w=W),
                                    window(start + PAIRS[u][0], PAIRS[u][1]), ALU.mult).then_inc(s_prod, 1)

                def own_sum(u):
                    after(dve, s_prod, TAPS, c, u + 1)
                    after(dve, s_accv, len(BY_VECTOR), c, BY_VECTOR.index(u))
                    v.tensor_tensor(acc_v[:], acc_v[:], prod_v[:], ALU.add).then_inc(s_accv, 1)

                def sum_x1(k):
                    if k == 0:
                        after(dve, s_accp, POOL_OPS, l, POOL_OPS)
                        after(dve, s_accv, len(BY_VECTOR), l, len(BY_VECTOR))
                        i = v.tensor_tensor(acc_v[:], acc_v[:], acc_p[:], ALU.add)
                    elif k == 1:
                        after(dve, s_x1, 3, l, 1)
                        after(dve, s_x1_res, 1, l, 0)
                        i = v.tensor_tensor(x1[:], acc_v[:, 0:N], acc_v[:, N:2 * N], ALU.add)
                    else:
                        after(dve, s_x1, 3, l, 2)
                        i = v.tensor_tensor(x1[:], x1[:], single[:], ALU.add)
                    i.then_inc(s_x1, 1)

                def gated(tile, e):
                    after(dve, s_w2, CH, tile, CPE * (e + 1))
                    after(dve, s_y, EXPERTS, tile, e - 1)
                    v.tensor_tensor(gy[:, e % 2, :], y_ps[:, 0:N], gate_b[:, e % 2, :], ALU.mult).then_inc(s_gy, 1)

                for j in range(STEPS):
                    if j == 0 and "ffn" in stages:
                        after(dve, s_xf_hi, 1, f, 1)
                        v.tensor_tensor(xf_lo[:], xn2[:], xf_hi[:].bitcast(F32), ALU.subtract).then_inc(s_xf_lo, 1)
                    if j == 0 and "conv" in stages:
                        dve.wait_ge(s_bank_out, bank_count(stages, base, "h"))
                        v.tensor_tensor(h_stack[RED:2 * RED, :], h_full[RED:2 * RED, :],
                                        h_stack[RED:2 * RED, :].bitcast(F32), ALU.subtract).then_inc(s_h_lo, 1)
                    if j == 1 and "tail" in stages:
                        dve.wait_ge(s_bank_out, base)
                        gated(f - 1, EXPERTS - 1)
                    if j >= 4 and (j - 4) % CPE == 0 and "ffn" in stages:
                        e = (j - 4) // CPE
                        dve.wait_ge(s_bank_out, bank_count(stages, base, f"gate{e}"))
                        gated(f, e)
                    if j == 1 and "ln2" in stages:
                        sum_x1(0)
                        sum_x1(1)
                        sum_x1(2)
                    if "conv" in stages:
                        for u in UNITS_AT[j]:
                            unit(u)
                    if "ln2" in stages:
                        if j in (4, 5):
                            ln("ln2", j - 4, "x1_t", LN_T_EPS)
                        if j == 6:
                            ln("ln2", 2, "x1_t", LN_T_EPS)
                        if j == 8:
                            ln("ln2", 3, "x1_t", LN_T_EPS)
                        if j == 13:
                            router_step(0)
                        if j == 14:
                            router_step(1)
                    if "ffn" in stages:
                        after(dve, s_silu, CH, f, j + 1)
                        after(dve, s_h3, CH, f, j + 1)
                        after(dve, s_w2, CH, f, j - 2)
                        v.tensor_tensor(hid[:, j % 3, :], silu[:, j % 2, :], h3_ps[0:HC, 0:N], ALU.mult).then_inc(s_hid, 1)
                    if "conv" in stages:
                        for u in UNITS_AT[j]:
                            if u in BY_VECTOR:
                                own_sum(u)
                    if "ln1" in stages:
                        if j in (5, 6, 7):
                            ln("ln1", j - 5, "x_t", LN_C_EPS)
                        if j == 9:
                            ln("ln1", 3, "x_t", LN_C_EPS)
                    if "ln2" in stages and j >= 18:
                        for k in range(2 + 3 * (j - 18), min(2 + 3 * (j - 17), RT)):
                            router_step(k)
                    if j == STEPS - 1 and "ln2" in stages:
                        dve.wait_ge(s_bank_out, bank_count(stages, base, "gates_t"))
                        v.tensor_tensor(gate_t[32:40, :], gate_f[32:40, :], gate_t[32:40, :].bitcast(F32),
                                        ALU.subtract).then_inc(s_gate_lo, 1)

            run(dve, body)

        @block.gpsimd
        def _(pool):
            g = nc.gpsimd
            g.memset(xn[:], 0.0).then_inc(s_setp, 1)
            g.memset(minus_half[:], -0.5)
            g.memset(euler[:], 2.718281828459045).then_inc(s_setp, 1)
            pool.wait_ge(s_setp, 2)
            pool.wait_ge(s_piece_lo, len(PIECES))

            def body(t, stages, base):
                f, c, l = t, t + AHEAD["conv"], t + AHEAD["ln2"]

                def rsqrt(stage):
                    after(pool, s_ln[stage], 4, t + AHEAD[stage], 3)
                    after(pool, s_tok[stage], 1, t + AHEAD[stage], 0)
                    g.tensor_tensor(rstd[stage][:], veps[stage][:], minus_half[:], ALU.pow).then_inc(s_rstd[stage], 1)

                def unit(u):
                    if u in BY_POOL:
                        after(pool, s_prod, TAPS, c, u + 1)
                        k = BY_POOL.index(u)
                        after(pool, s_accp, POOL_OPS, c, k)
                        g.tensor_tensor(acc_p[:], acc_p[:], prod[:, k % PRING, :], ALU.add).then_inc(s_accp, 1)
                    elif u == TAPS - 1:
                        after(pool, s_prod, TAPS, c, TAPS)
                        after(pool, s_x_res, 16, c, 16)
                        after(pool, s_x1, 3, c, 0)
                        g.tensor_tensor(single[:], x_res[:], prod[:, (POOL_OPS - 1) % PRING, 0:N], ALU.add).then_inc(s_accp, 1)

                def add_expert(tile, e):
                    after(pool, s_gy, EXPERTS, tile, e + 1)
                    after(pool, s_y, EXPERTS, tile, e)
                    if e == 0:
                        after(pool, s_x1_res, 1, tile, 1)
                        i = g.tensor_tensor(y_acc[:], x1_res[:], gy[:, 0, :], ALU.add)
                    elif e < EXPERTS - 1:
                        i = g.tensor_tensor(y_acc[:], y_acc[:], gy[:, e % 2, :], ALU.add)
                    else:
                        after(pool, s_out, 16, tile, 0)
                        i = g.tensor_tensor(y_out[:], y_acc[:], gy[:, e % 2, :], ALU.add)
                    i.then_inc(s_y, 1)

                for j in range(STEPS):
                    if j == 1 and "tail" in stages:
                        add_expert(f - 1, EXPERTS - 1)
                    if j >= 4 and (j - 4) % CPE == 0 and "ffn" in stages:
                        add_expert(f, (j - 4) // CPE)
                    if j == 7 and "ln2" in stages:
                        rsqrt("ln2")
                    if j == 8 and "ln1" in stages:
                        rsqrt("ln1")
                    if "conv" in stages:
                        for u in UNITS_AT[j]:
                            unit(u)
                    if j == 15 and "ln2" in stages:
                        after(pool, s_rt, RT, l, 2)
                        g.tensor_tensor(lexp[:].rearrange("p a b -> p (a b)"), euler[:],
                                        ldiff[:].rearrange("p a b -> p (a b)"), ALU.pow).then_inc(s_exp, 1)

            run(pool, body)


def kernel(x, L0_conv_reduce_w, L0_conv_reduce_b, L0_conv_span_w, L0_conv_span_b, L0_ffn_router_w,
           L0_ffn_w1, L0_ffn_w2, L0_ffn_w3):
    import numpy as np
    import concourse.bacc as bacc
    from concourse.bass_utils import run_bass_kernel_spmd

    f = np.float32
    x = np.asarray(x)
    xt = np.ascontiguousarray(x.reshape(B, C, H * W).transpose(1, 0, 2).reshape(C, B * H * W))
    w_red = np.ascontiguousarray(np.tile(np.asarray(L0_conv_reduce_w).T, (1, 3)))
    b_red = np.ascontiguousarray(np.tile(np.asarray(L0_conv_reduce_b), 3).reshape(3 * RED, 1))
    sw = np.asarray(L0_conv_span_w).reshape(GROUPS, KS * KS, RED)[:, TAP_ORDER, :]
    sw = np.repeat(sw.transpose(2, 1, 0), C // GROUPS, axis=2).reshape(RED, KS * KS * C)
    sbias = np.asarray(L0_conv_span_b).reshape(GROUPS, KS * KS)[:, TAP_ORDER]
    sbias = np.repeat(sbias.T, C // GROUPS, axis=1).reshape(1, KS * KS * C)
    w_span = np.ascontiguousarray(np.concatenate([sw, sw, sw, sbias, sbias], axis=0))

    def chunks(w):
        p = np.zeros((EXPERTS, CPE * HC, C), f)
        p[:, :HID] = w
        return p.reshape(CH, HC, C)

    w1 = np.ascontiguousarray(chunks(np.asarray(L0_ffn_w1)).reshape(CH * HC, C).T)
    w3 = np.ascontiguousarray(chunks(np.asarray(L0_ffn_w3)).reshape(CH * HC, C).T)
    w2 = np.ascontiguousarray(chunks(np.asarray(L0_ffn_w2).transpose(0, 2, 1)).transpose(1, 0, 2).reshape(HC, CH * C))
    select = np.zeros((40, EXPERTS, C), f)
    for e in range(EXPERTS):
        select[e, e] = 1.0
        select[32 + e, e] = 1.0
    arrays = {
        "x": xt, "w_red": w_red, "b_red": b_red, "w_span": w_span,
        "router": np.ascontiguousarray(np.asarray(L0_ffn_router_w).T), "w1": w1, "w3": w3, "w2": w2,
        "ident": np.eye(C, dtype=f), "select": select.reshape(40, EXPERTS * C),
        "iota": np.ascontiguousarray(np.broadcast_to(np.tile(np.arange(EXPERTS, dtype=f), SUBS), (SUB, SUBS * EXPERTS))),
    }
    nc = bacc.Bacc("TRN2", target_bir_lowering=False, num_devices=1)
    args = [nc.dram_tensor(f"in_{n}", a.shape, mybir.dt.from_np(a.dtype), kind="ExternalInput").ap() for n, a in arrays.items()]
    out = nc.dram_tensor("out", (C, B * H * W), F32, kind="ExternalOutput").ap()
    build(nc, *args, out)
    r = run_bass_kernel_spmd(nc, [{f"in_{n}": a for n, a in arrays.items()}], core_ids=[0])
    got = r.results[0]["out"]
    return np.ascontiguousarray(got.reshape(C, B, H * W).transpose(1, 0, 2).reshape(B, C, H, W))
```

```python
from contextlib import ExitStack

import concourse.bass as bass
from concourse import mybir

F32 = mybir.dt.float32
F32R = mybir.dt.float32r
U32 = mybir.dt.uint32
ALU = mybir.AluOpType
ACT = mybir.ActivationFunctionType
AX = mybir.AxisListType.X

B, C, H, W = 4, 128, 56, 56
GROUPS, KS, PAD, RED = 16, 7, 3, 32
EXPERTS, HID = 8, 341
LN_C_EPS, LN_T_EPS, GATE_EPS = 1e-6, 1e-5, 1e-9

ROWS = 8
N = ROWS * W
SUBS, SUB = 4, N // 4
PER_IMG = H // ROWS
TILES = B * PER_IMG
PW = W + 2 * PAD
IMG = (H + 2 * PAD) * PW

CPE = 3
HC = -(-HID // CPE)
CH = EXPERTS * CPE

PAIRS = [(dy * PW + dx, 1) for dy in range(KS) for dx in (0, 2, 4)] + [(dy * PW + 6, PW) for dy in (0, 2, 4)]
SINGLE = 6 * PW + 6
TAPS = len(PAIRS) + 1
TAP_ORDER = [(dy * KS + dx + i) for dy in range(KS) for dx in (0, 2, 4) for i in (0, 1)] + [
    (dy + i) * KS + 6 for dy in (0, 2, 4) for i in (0, 1)] + [KS * KS - 1]

BY_VECTOR = (3, 7, 11, 15, 19, 22)
BY_POOL = [u for u in range(TAPS - 1) if u not in BY_VECTOR]
V_SUMS = len(BY_VECTOR) - 1
PRING = 5
HR = 3
POOL_OPS = len(BY_POOL) - 1 + 2

GW = 72

STEPS = CH
UNITS_AT = {s: [] for s in range(STEPS)}
_u = 0
for _s in range(STEPS):
    for _ in range(2 if _s == 12 else 1):
        UNITS_AT[_s].append(_u)
        _u += 1
assert _u == TAPS
LAG = 3

BANK_AT = {s: [] for s in range(STEPS)}
for _s, _use in ((0, ("ln1", "x_t")), (1, ("ffn", "gates_t")), (4, ("ln2", "x1_t")), (10, ("ln1", "xn")),
                 (12, ("ln2", "xn2")), (13, ("ln2", "logits")), (21, ("reduce", "h"))):
    BANK_AT[_s].append(_use)
for _e, _s in enumerate((3, 6, 9, 14, 15, 18, 20, 22)):
    BANK_AT[_s].append(("ffn", f"gate{_e}"))

AHEAD = {"ln1": 4, "reduce": 3, "conv": 2, "ln2": 1, "ffn": 0, "tail": -1}


def bodies():
    out = []
    for t in range(-4, TILES + 1):
        stages = tuple(s for s, a in AHEAD.items() if 0 <= t + a < TILES)
        first = any(t + a == 0 for a in AHEAD.values())
        if out and out[-1][2] == stages and not out[-1][3] and not first:
            out[-1][1] = t + 1
        else:
            out.append([t, t + 1, stages, first])
    return [(a, b, s) for a, b, s, _ in out]


def bank_uses(stages):
    return [name for s in range(STEPS) for stage, name in BANK_AT[s] if stage in stages]


def build(nc, x, w_red, b_red, w_span, router, w1, w3, w2, ident, select, iota, out):
    with ExitStack() as ctx:
        def sb(name, shape, dt=F32):
            return ctx.enter_context(nc.sbuf_tensor(name, shape, dt))

        def psum(name, shape):
            return ctx.enter_context(nc.psum_tensor(name, shape, F32))

        def sem(name):
            return ctx.enter_context(nc.semaphore(name))

        kern_ps = psum("kern_ps", [C, 2, 2, 512])
        h1_ps = psum("h1_ps", [C, 512])
        h3_ps = psum("h3_ps", [C, 512])
        y_ps = psum("y_ps", [C, 512])
        bank = psum("bank", [C, 512])

        w1_hi, w1_lo = sb("w1_hi", [C, CH * HC], F32R), sb("w1_lo", [C, CH * HC], F32R)
        w3_hi, w3_lo = sb("w3_hi", [C, CH * HC], F32R), sb("w3_lo", [C, CH * HC], F32R)
        w2_sb = sb("w2_sb", [HC, CH, C])
        span = sb("span", [98, KS * KS * C], F32R)
        red_sb = sb("red_sb", [C, 3 * RED])
        bred_sb = sb("bred_sb", [3 * RED, 1])
        router_sb = sb("router_sb", [C, EXPERTS])
        ident_sb = sb("ident_sb", [C, C])
        select_raw = sb("select_raw", [40, EXPERTS * C])
        select_sb = sb("select_sb", [40, EXPERTS * C], F32R)
        iota_sb = sb("iota_sb", [SUB, SUBS, EXPERTS])
        minus_half = sb("minus_half", [SUB, SUBS])
        euler = sb("euler", [SUB, SUBS * EXPERTS])

        xn = sb("xn", [C, 2 * IMG])
        x_ln = sb("x_ln", [C, N])
        x_res = sb("x_res", [C, N])
        h_stack = sb("h_stack", [98, N], F32R)
        h_full = sb("h_full", [3 * RED, N])
        prod = sb("prod", [C, PRING, 2 * N])
        prod_v = sb("prod_v", [C, 2 * N])
        acc_p = sb("acc_p", [C, 2 * N])
        acc_v = sb("acc_v", [C, 2 * N])
        single = sb("single", [C, N])

        tok = {k: sb(f"tok_{k}", [SUB, SUBS, C]) for k in ("ln1", "ln2")}
        stats = {k: sb(f"stats_{k}", [SUB, SUBS, 6]) for k in ("ln1", "ln2")}
        mv = {k: sb(f"mv_{k}", [SUB, SUBS, 2]) for k in ("ln1", "ln2")}
        veps = {k: sb(f"veps_{k}", [SUB, SUBS]) for k in ("ln1", "ln2")}
        rstd = {k: sb(f"rstd_{k}", [SUB, SUBS]) for k in ("ln1", "ln2")}
        shift = {k: sb(f"shift_{k}", [SUB, SUBS]) for k in ("ln1", "ln2")}
        logits = sb("logits", [SUB, SUBS, EXPERTS])
        lmax = sb("lmax", [SUB, SUBS])
        ldiff = sb("ldiff", [SUB, SUBS, EXPERTS])
        lexp = sb("lexp", [SUB, SUBS, EXPERTS])
        lsum = sb("lsum", [SUB, SUBS])
        rsum = sb("rsum", [SUB, SUBS])
        probs = sb("probs", [SUB, SUBS, EXPERTS])
        top = sb("top", [SUB, SUBS, EXPERTS])
        top_at = sb("top_at", [SUB, SUBS, EXPERTS], U32)
        top_atf = sb("top_atf", [SUB, SUBS, 2])
        gden = sb("gden", [SUB, SUBS])
        grec = sb("grec", [SUB, SUBS])
        gtop = sb("gtop", [SUB, SUBS, 2])
        hot = sb("hot", [SUB, SUBS, 2, EXPERTS])
        gates = sb("gates", [SUB, SUBS, GW])
        gate_t = sb("gate_t", [40, N], F32R)
        gate_f = sb("gate_f", [40, N])

        nothing = sb("nothing", [1, 1])

        x1 = sb("x1", [C, N])
        x1_p = sb("x1_p", [C, N])
        x1_res = sb("x1_res", [C, N])
        xn2 = sb("xn2", [C, N])
        xf_hi, xf_lo = sb("xf_hi", [C, N], F32R), sb("xf_lo", [C, N], F32R)
        silu = sb("silu", [HC, HR, N])
        h3_sb = sb("h3_sb", [HC, HR, N])
        hid = sb("hid", [HC, HR, N])
        gate_b = sb("gate_b", [C, 2, N])
        y_sb = sb("y_sb", [C, 2, N])
        gy = sb("gy", [C, 2, N])
        y_acc = sb("y_acc", [C, N])
        y_out = sb("y_out", [C, N])

        s_const = sem("s_const")
        s_w2_in = sem("s_w2_in")
        s_stage = [sem(f"s_stage{i}") for i in range(PRING)]
        s_piece_hi = sem("s_piece_hi")
        s_piece_lo = sem("s_piece_lo")
        s_set = sem("s_set")
        s_setp = sem("s_setp")
        s_sel = sem("s_sel")
        s_bank = sem("s_bank")
        s_bank_out = sem("s_bank_out")
        s_x_ln = sem("s_x_ln")
        s_x_res = sem("s_x_res")
        s_ln = {k: sem(f"s_{k}_v") for k in ("ln1", "ln2")}
        s_rstd = {k: sem(f"s_{k}_rstd") for k in ("ln1", "ln2")}
        s_tok = {k: sem(f"s_{k}_tok") for k in ("ln1", "ln2")}
        s_h_lo = sem("s_h_lo")
        s_kern = sem("s_kern")
        s_prod = sem("s_prod")
        s_accv = sem("s_accv")
        s_accp = sem("s_accp")
        s_x1 = sem("s_x1")
        s_x1_res = sem("s_x1_res")
        s_rt = sem("s_rt")
        s_exp = sem("s_exp")
        s_gate_lo = sem("s_gate_lo")
        s_xf_hi = sem("s_xf_hi")
        s_xf_lo = sem("s_xf_lo")
        s_h1 = sem("s_h1")
        s_silu = sem("s_silu")
        s_h3 = sem("s_h3")
        s_h3_out = sem("s_h3_out")
        s_h_hi = sem("s_h_hi")
        s_hid = sem("s_hid")
        s_w2 = sem("s_w2")
        s_y_out = sem("s_y_out")
        s_gy = sem("s_gy")
        s_y = sem("s_y")
        s_out = sem("s_out")

        RT = 14
        NCONST = 6

        span_pieces = [("span", i) for i in range(KS)]
        w_pieces = [(w, i) for w in ("w1", "w3") for i in range(4)]
        PIECES = span_pieces + w_pieces
        WCOLS = CH * HC // 4
        SCOLS = KS * C

        def w_pieces_in(t):
            if isinstance(t, int) and t in (-4, -3):
                n = len(w_pieces) // 2
                return range(len(span_pieces) + (t + 4) * n, len(span_pieces) + (t + 5) * n)
            return range(0)

        def after(eng, s, per, tile, k):
            v = tile * per + k
            if not isinstance(v, int) or v > 0:
                eng.wait_ge(s, v)

        def after_apart(s, per, tile, k):
            after(nc.vector, s, per, tile, k)
            nc.vector.memset(nothing[:], 0.0)

        def run(eng, body):
            base = 0
            for first, end, stages in bodies():
                uses = len(bank_uses(stages))
                if end - first == 1:
                    body(first, stages, base)
                else:
                    with eng.Fori(first, end) as t:
                        body(t, stages, (t - first) * uses + base)
                base += uses * (end - first)

        def bank_count(stages, base, name):
            return base + bank_uses(stages).index(name) + 1

        def xn_at(tile):
            return ((tile // PER_IMG) % 2) * IMG + (tile % PER_IMG) * (ROWS * PW)

        def window(start, pair_step=None):
            pdim = list(xn[:, 0:1].ap[0])
            dims = ([[pair_step, 2]] if pair_step else []) + [[PW, ROWS], [1, W]]
            return bass.AP(tensor=xn[:, 0:1].tensor, offset=start, ap=[pdim] + dims)

        def rows(ap):
            return ap.rearrange("p (r w) -> p r w", w=W)

        def pair_rows(ap):
            return ap.rearrange("p (i r w) -> p i r w", i=2, w=W)

        block = ctx.enter_context(nc.Block())

        @block.sync
        def _(sp):
            for dst, src in ((ident_sb[:], ident), (red_sb[:], w_red), (bred_sb[:], b_red), (router_sb[:], router),
                             (select_raw[:], select), (iota_sb[:].rearrange("p a b -> p (a b)"), iota)):
                sp.dma_start(dst, src).then_inc(s_const, 16)

            def load_piece(i):
                kind, k = PIECES[i]
                if i >= PRING:
                    sp.wait_ge(s_piece_lo, i - PRING + 1)
                if kind == "span":
                    sp.dma_start(prod[0:98, i % PRING, 0:SCOLS], w_span[:, k * SCOLS:(k + 1) * SCOLS]).then_inc(s_stage[i % PRING], 16)
                else:
                    src = (w1 if kind == "w1" else w3)[:, k * WCOLS:(k + 1) * WCOLS]
                    sp.dma_start(prod[:, i % PRING, 0:WCOLS], src).then_inc(s_stage[i % PRING], 16)
            for i in range(len(span_pieces)):
                load_piece(i)

            def body(t, stages, base):
                if "ln1" in stages:
                    after(sp, s_tok["ln1"], 1, t + AHEAD["ln1"], 0)
                    sp.dma_start(x_ln[:], x[:, bass.ds((t + AHEAD["ln1"]) * N, N)]).then_inc(s_x_ln, 16)
                for i in w_pieces_in(t):
                    load_piece(i)
                if isinstance(t, int) and t == -3:
                    sp.dma_start(w2_sb[:].rearrange("p a b -> p (a b)"), w2).then_inc(s_w2_in, 16)
                if "conv" in stages:
                    after(sp, s_accp, POOL_OPS, t + AHEAD["conv"], 0)
                    sp.dma_start(x_res[:], x[:, bass.ds((t + AHEAD["conv"]) * N, N)]).then_inc(s_x_res, 16)
                if "tail" in stages:
                    after(sp, s_y, EXPERTS, t - 1, EXPERTS)
                    sp.dma_start(out[:, bass.ds((t - 1) * N, N)], y_out[:]).then_inc(s_out, 16)

            run(sp, body)
            sp.wait_ge(s_out, 16 * TILES)

        @block.tensor
        def _(pe):
            mm = nc.tensor.matmul

            def body(t, stages, base):
                f, c = t, t + AHEAD["conv"]
                used = [0]

                def take_bank():
                    v = base + used[0]
                    if not isinstance(v, int) or v > 0:
                        pe.wait_ge(s_bank_out, v)
                    used[0] += 1

                def bank_use(stage, name):
                    take_bank()
                    if name == "h":
                        i = mm(bank[0:3 * RED, 0:N], red_sb[:], window(xn_at(t + AHEAD["reduce"]) + PAD * PW + PAD), start=True, stop=True)
                    elif name in ("x_t", "x1_t"):
                        if name == "x_t":
                            after(pe, s_x_ln, 16, t + AHEAD["ln1"], 16)
                        else:
                            after(pe, s_x1, 3, t + AHEAD["ln2"], 3)
                        src = x_ln if name == "x_t" else x1
                        for k in range(SUBS):
                            i = nc.tensor.transpose(bank[0:SUB, k * C:(k + 1) * C], src[:, k * SUB:(k + 1) * SUB], ident_sb[:])
                    elif name in ("xn", "xn2"):
                        after(pe, s_tok[stage], 1, t + AHEAD[stage], 1)
                        for k in range(SUBS):
                            i = nc.tensor.transpose(bank[:, k * SUB:(k + 1) * SUB], tok[stage][:, k, :], ident_sb[0:SUB, 0:SUB])
                    elif name == "logits":
                        for k in range(SUBS):
                            i = mm(bank[0:SUB, k * EXPERTS:(k + 1) * EXPERTS], xn2[:, k * SUB:(k + 1) * SUB], router_sb[:],
                                   start=True, stop=True)
                    elif name == "gates_t":
                        after(pe, s_rt, RT, f, RT)
                        for k in range(SUBS):
                            i = nc.tensor.transpose(bank[0:GW, k * SUB:(k + 1) * SUB], gates[:, k, :], ident_sb[0:SUB, 0:SUB])
                    else:
                        e = int(name[4:])
                        if e == 0:
                            after(pe, s_gate_lo, 1, f, 1)
                        i = mm(bank[:, 0:N], select_sb[:, e * C:(e + 1) * C], gate_t[:], start=True, stop=True)
                    i.then_inc(s_bank, 1)

                def unit(u):
                    if u == 0:
                        after(pe, s_h_lo, 1, c, 1)
                        after(pe, s_prod, TAPS, c, 0)
                    elif u >= 2:
                        after(pe, s_prod, TAPS, c, u - 1)
                    for i in range(2 if u < TAPS - 1 else 1):
                        k = 2 * u + i
                        last = mm(kern_ps[:, u % 2, i, 0:N], span[:, k * C:(k + 1) * C], h_stack[:], start=True, stop=True)
                    last.then_inc(s_kern, 1)

                def hidden(j, ps, hi, lo, done):
                    a, b = j * HC, (j + 1) * HC
                    if j == 0:
                        after(pe, s_xf_hi, 1, f, 1)
                    mm(ps[0:HC, 0:N], lo[:, a:b], xf_hi[:], start=True, stop=False)
                    mm(ps[0:HC, 0:N], hi[:, a:b], xf_hi[:], start=False, stop=False)
                    if j == 0:
                        after(pe, s_xf_lo, 1, f, 1)
                    mm(ps[0:HC, 0:N], hi[:, a:b], xf_lo[:], start=False, stop=True).then_inc(done, 1)

                def down(tile, j):
                    after(pe, s_hid, CH, tile, j + 1)
                    if j % CPE == 0:
                        after(pe, s_y_out, EXPERTS, tile, j // CPE)
                    mm(y_ps[:, 0:N], w2_sb[:, j, :], hid[:, j % HR, :], start=j % CPE == 0,
                       stop=j % CPE == CPE - 1).then_inc(s_w2, 1)

                if isinstance(t, int) and t == 0:
                    pe.wait_ge(s_piece_lo, len(PIECES))
                    pe.wait_ge(s_w2_in, 16)
                for j in range(STEPS):
                    at_end = j in (0, STEPS - 1)
                    if j < LAG and "tail" in stages:
                        down(f - 1, CH - LAG + j)
                    if j == STEPS - 1 and "ffn" in stages:
                        down(f, j - LAG)
                    if j == 0 and "ln1" in stages:
                        bank_use("ln1", "x_t")
                    if "ffn" in stages:
                        after(pe, s_silu, CH, f, j)
                        hidden(j, h1_ps, w1_hi, w1_lo, s_h1)
                        if at_end:
                            after(pe, s_h3_out, CH, f, j)
                            hidden(j, h3_ps, w3_hi, w3_lo, s_h3)
                    if "conv" in stages:
                        for u in UNITS_AT[j]:
                            unit(u)
                    if "ffn" in stages and not at_end:
                        if j >= LAG:
                            down(f, j - LAG)
                        after(pe, s_h3_out, CH, f, j)
                        hidden(j, h3_ps, w3_hi, w3_lo, s_h3)
                    for stage, name in BANK_AT[j]:
                        if stage in stages and name != "x_t":
                            bank_use(stage, name)

            pe.wait_ge(s_const, 16 * NCONST)
            pe.wait_ge(s_sel, 1)
            pe.wait_ge(s_set, 2)
            pe.wait_ge(s_setp, 2)
            pe.wait_ge(s_piece_lo, len(span_pieces))
            run(pe, body)

        @block.scalar
        def _(act):
            act_f = nc.scalar.activation

            def high_parts(i):
                kind, k = PIECES[i]
                act.wait_ge(s_stage[i % PRING], 16 * (i // PRING + 1))
                if kind == "span":
                    act_f(span[:, k * SCOLS:(k + 1) * SCOLS], prod[0:98, i % PRING, 0:SCOLS], ACT.Copy).then_inc(s_piece_hi, 1)
                else:
                    dst = (w1_hi if kind == "w1" else w3_hi)[:, k * WCOLS:(k + 1) * WCOLS]
                    act_f(dst, prod[:, i % PRING, 0:WCOLS], ACT.Copy).then_inc(s_piece_hi, 1)

            for i in range(len(span_pieces)):
                high_parts(i)
            act.wait_ge(s_const, 16 * NCONST)
            act_f(select_sb[:], select_raw[:], ACT.Copy).then_inc(s_sel, 1)
            act.wait_ge(s_setp, 2)

            def body(t, stages, base):
                f, c = t, t + AHEAD["conv"]
                used = [0]

                def bank_use(stage, name):
                    used[0] += 1
                    act.wait_ge(s_bank, base + used[0])
                    if name == "h":
                        after(act, s_h_lo, 1, t + AHEAD["reduce"], 0)
                        i = act_f(h_full[:], bank[0:3 * RED, 0:N], ACT.Identity, bias=bred_sb[:, 0:1])
                    elif name in ("x_t", "x1_t"):
                        i = act_f(tok[stage][:], bank[0:SUB, :].rearrange("p (a b) -> p a b", a=SUBS), ACT.Copy)
                    elif name == "xn":
                        dst = window(xn_at(t + AHEAD["ln1"]) + PAD * PW + PAD)
                        i = act_f(dst, rows(bank[:, 0:N]), ACT.Copy)
                    elif name == "xn2":
                        after(act, s_xf_lo, 1, t + AHEAD["ln2"], 0)
                        i = act_f(xn2[:], bank[:, 0:N], ACT.Copy)
                    elif name == "logits":
                        i = act_f(logits[:], bank[0:SUB, 0:SUBS * EXPERTS].rearrange("p (a b) -> p a b", a=SUBS), ACT.Copy)
                    elif name == "gates_t":
                        act_f(gate_f[:], bank[0:40, 0:N], ACT.Copy)
                        i = act_f(gate_t[:], bank[0:40, 0:N], ACT.Copy)
                    else:
                        e = int(name[4:])
                        after(act, s_gy, EXPERTS, f, e - 1)
                        i = act_f(gate_b[:, e % 2, :], bank[:, 0:N], ACT.Copy)
                    i.then_inc(s_bank_out, 1)

                def copy_y(tile, e):
                    after(act, s_w2, CH, tile, CPE * (e + 1))
                    after(act, s_gy, EXPERTS, tile, e - 1)
                    act_f(y_sb[:, e % 2, :], y_ps[:, 0:N], ACT.Copy).then_inc(s_y_out, 1)

                def normalise(stage, tile, half):
                    after(act, s_ln[stage], 4, tile, 4)
                    for k in (2 * half, 2 * half + 1):
                        i = act_f(tok[stage][:, k, :], tok[stage][:, k, :], ACT.Identity,
                                  bias=shift[stage][:, k:k + 1], scale=rstd[stage][:, k:k + 1])
                    if half:
                        i.then_inc(s_tok[stage], 1)

                for j in range(STEPS):
                    if j == 0 and "ffn" in stages:
                        after(act, s_h3, CH, f, 0)
                        act_f(xf_hi[:], xn2[:], ACT.Copy).then_inc(s_xf_hi, 1)
                    if j == 0 and "conv" in stages:
                        after(act, s_kern, TAPS, c, 0)
                        act.wait_ge(s_bank_out, base)
                        act_f(h_stack[0:3 * RED, :], h_full[:], ACT.Copy).then_inc(s_h_hi, 1)
                    if j == STEPS - 1 and "ffn" in stages:
                        copy_y(f, EXPERTS - 2)
                    if "ffn" in stages:
                        after(act, s_h1, CH, f, j + 1)
                        after(act, s_hid, CH, f, j + 1 - HR)
                        act_f(silu[:, j % HR, :], h1_ps[0:HC, 0:N], ACT.Silu).then_inc(s_silu, 1)
                    if j < LAG and j == LAG - 1 and "tail" in stages:
                        copy_y(f - 1, EXPERTS - 1)
                    if LAG <= j < STEPS - 1 and (j - LAG) % CPE == CPE - 1 and "ffn" in stages:
                        copy_y(f, (j - LAG) // CPE)
                    if "ffn" in stages:
                        after(act, s_h3, CH, f, j + 1)
                        act_f(h3_sb[:, j % HR, :], h3_ps[0:HC, 0:N], ACT.Copy).then_inc(s_h3_out, 1)
                    for stage, name in BANK_AT[j]:
                        if stage in stages:
                            bank_use(stage, name)
                    if j == 6:
                        for i in w_pieces_in(t):
                            high_parts(i)
                    if j in (10, 11) and "ln2" in stages:
                        normalise("ln2", t + AHEAD["ln2"], j - 10)
                    if j in (8, 9) and "ln1" in stages:
                        normalise("ln1", t + AHEAD["ln1"], j - 8)
                    if j == 19 and "ln2" in stages:
                        after(act, s_y, EXPERTS, t, 1)
                        act_f(x1_res[:], x1[:], ACT.Copy).then_inc(s_x1_res, 1)

            run(act, body)

        @block.vector
        def _(dve):
            v = nc.vector
            v.memset(h_stack[96:98, :].bitcast(F32), 1.0).then_inc(s_set, 1)
            v.memset(gates[:], 0.0).then_inc(s_set, 1)

            def low_parts(i):
                kind, k = PIECES[i]
                dve.wait_ge(s_stage[i % PRING], 16 * (i // PRING + 1))
                dve.wait_ge(s_piece_hi, i + 1)
                if kind == "span":
                    hi = span[64:97, k * SCOLS:(k + 1) * SCOLS]
                    v.tensor_tensor(hi, prod[64:97, i % PRING, 0:SCOLS], hi.bitcast(F32), ALU.subtract).then_inc(s_piece_lo, 1)
                else:
                    hi, lo = (w1_hi, w1_lo) if kind == "w1" else (w3_hi, w3_lo)
                    v.tensor_tensor(lo[:, k * WCOLS:(k + 1) * WCOLS], prod[:, i % PRING, 0:WCOLS],
                                    hi[:, k * WCOLS:(k + 1) * WCOLS].bitcast(F32), ALU.subtract).then_inc(s_piece_lo, 1)

            for i in range(len(span_pieces)):
                low_parts(i)
            dve.wait_ge(s_const, 16 * NCONST)
            dve.wait_ge(s_set, 2)
            dve.wait_ge(s_setp, 2)

            def body(t, stages, base):
                f, c, l = t, t + AHEAD["conv"], t + AHEAD["ln2"]

                def ln(stage, k, name, eps):
                    tile = t + AHEAD[stage]
                    if k == 0:
                        dve.wait_ge(s_bank_out, bank_count(stages, base, name))
                        for q in range(SUBS):
                            i = v.bn_stats(stats[stage][:, q, :], tok[stage][:, q, :])
                    elif k == 1:
                        after_apart(s_ln[stage], 4, tile, 1)
                        for q in range(SUBS):
                            i = v.bn_aggr(mv[stage][:, q, :], stats[stage][:, q, :])
                    elif k == 2:
                        after(dve, s_ln[stage], 4, tile, 2)
                        i = v.tensor_scalar(veps[stage][:], mv[stage][:, :, 1], eps, None, ALU.add)
                    else:
                        after(dve, s_rstd[stage], 1, tile, 1)
                        i = v.scalar_tensor_tensor(out=shift[stage][:], in0=mv[stage][:, :, 0], scalar=-1.0,
                                                   in1=rstd[stage][:], op0=ALU.mult, op1=ALU.mult)
                    i.then_inc(s_ln[stage], 1)

                EACH = [SUB, SUBS, 2, EXPERTS]

                def router_step(k):
                    if k == 0:
                        dve.wait_ge(s_bank_out, bank_count(stages, base, "logits"))
                        i = v.tensor_reduce(lmax[:], logits[:], AX, ALU.max)
                    elif k == 2:
                        after(dve, s_exp, SUBS, l, SUBS)
                        i = v.tensor_reduce(lsum[:], lexp[:], AX, ALU.add)
                    else:
                        if k in (5, 6):
                            after_apart(s_rt, RT, l, k)
                        else:
                            after(dve, s_rt, RT, l, k)
                    if k == 1:
                        i = v.tensor_tensor(ldiff[:], logits[:], lmax[:].unsqueeze(2).broadcast_to([SUB, SUBS, EXPERTS]), ALU.subtract)
                    elif k == 3:
                        i = v.reciprocal(rsum[:], lsum[:])
                    elif k == 4:
                        i = v.tensor_tensor(probs[:], lexp[:], rsum[:].unsqueeze(2).broadcast_to([SUB, SUBS, EXPERTS]), ALU.mult)
                    elif k == 5:
                        for q in range(SUBS):
                            i = v.max(top[:, q, :], probs[:, q, :])
                    elif k == 6:
                        for q in range(SUBS):
                            i = v.max_index(top_at[:, q, :], top[:, q, :], probs[:, q, :])
                    elif k == 7:
                        i = v.tensor_copy(top_atf[:], top_at[:, :, 0:2])
                    elif k == 8:
                        i = v.scalar_tensor_tensor(out=gden[:], in0=top[:, :, 0], scalar=GATE_EPS, in1=top[:, :, 1],
                                                   op0=ALU.add, op1=ALU.add)
                    elif k == 9:
                        i = v.reciprocal(grec[:], gden[:])
                    elif k == 10:
                        i = v.tensor_tensor(gtop[:], top[:, :, 0:2], grec[:].unsqueeze(2).broadcast_to([SUB, SUBS, 2]), ALU.mult)
                    elif k == 11:
                        i = v.tensor_tensor(hot[:], iota_sb[:].unsqueeze(2).broadcast_to(EACH),
                                            top_atf[:].unsqueeze(3).broadcast_to(EACH), ALU.is_equal)
                    elif k == 12:
                        i = v.tensor_tensor(hot[:], hot[:], gtop[:].unsqueeze(3).broadcast_to(EACH), ALU.mult)
                    elif k == 13:
                        i = v.tensor_tensor(gates[:, :, 0:64].rearrange("p s (i c) -> p s i c", i=2)[:, :, :, 0:EXPERTS],
                                            hot[:, :, 0:1, :].broadcast_to(EACH), hot[:, :, 1:2, :].broadcast_to(EACH), ALU.add)
                    i.then_inc(s_rt, 1)

                def unit(u):
                    after(dve, s_kern, TAPS, c, u + 1)
                    start = xn_at(c)
                    if u in BY_VECTOR:
                        k = BY_VECTOR.index(u)
                        dst = prod_v if k else acc_v
                        if k:
                            after(dve, s_accv, V_SUMS, c, k - 1)
                        else:
                            after(dve, s_x1, 3, c - 1, 1)
                        dst = dst[:]
                    else:
                        k = BY_POOL.index(u) if u < TAPS - 1 else len(BY_POOL)
                        if k >= PRING:
                            after(dve, s_accp, POOL_OPS, c, max(k - PRING, 1))
                        else:
                            after(dve, s_accp, POOL_OPS, c - 1, max(i for i in range(len(BY_POOL) + 1) if i % PRING == k))
                        dst = prod[:, k % PRING, :]
                    if u == TAPS - 1:
                        v.tensor_tensor(rows(dst[:, 0:N]), rows(kern_ps[:, u % 2, 0, 0:N]),
                                        window(start + SINGLE), ALU.mult).then_inc(s_prod, 1)
                        return
                    v.tensor_tensor(pair_rows(dst), kern_ps[:, u % 2, :, 0:N].rearrange("p i (r w) -> p i r w", w=W),
                                    window(start + PAIRS[u][0], PAIRS[u][1]), ALU.mult).then_inc(s_prod, 1)

                def own_sum(u):
                    after(dve, s_prod, TAPS, c, u + 1)
                    after(dve, s_accv, V_SUMS, c, BY_VECTOR.index(u) - 1)
                    v.tensor_tensor(acc_v[:], acc_v[:], prod_v[:], ALU.add).then_inc(s_accv, 1)

                def sum_x1(k):
                    if k == 0:
                        after(dve, s_accv, V_SUMS, l, V_SUMS)
                        after(dve, s_x1_res, 1, l, 0)
                        i = v.tensor_tensor(x1[:], acc_v[:, 0:N], acc_v[:, N:2 * N], ALU.add)
                    else:
                        after(dve, s_accp, POOL_OPS, l, POOL_OPS)
                        after(dve, s_x1, 3, l, k)
                        i = v.tensor_tensor(x1[:], x1[:], (single, x1_p)[k - 1][:], ALU.add)
                    i.then_inc(s_x1, 1)

                def gated(tile, e):
                    after(dve, s_y_out, EXPERTS, tile, e + 1)
                    after(dve, s_y, EXPERTS, tile, e - 1)
                    v.tensor_tensor(gy[:, e % 2, :], y_sb[:, e % 2, :], gate_b[:, e % 2, :], ALU.mult).then_inc(s_gy, 1)

                def hidden(tile, j):
                    after(dve, s_silu, CH, tile, j + 1)
                    after(dve, s_h3_out, CH, tile, j + 1)
                    after(dve, s_w2, CH, tile, j + 1 - HR)
                    v.tensor_tensor(hid[:, j % HR, :], silu[:, j % HR, :], h3_sb[:, j % HR, :], ALU.mult).then_inc(s_hid, 1)

                for j in range(STEPS):
                    if j == 0 and "ffn" in stages:
                        after(dve, s_xf_hi, 1, f, 1)
                        v.tensor_tensor(xf_lo[:], xn2[:], xf_hi[:].bitcast(F32), ALU.subtract).then_inc(s_xf_lo, 1)
                    if j == 0 and "tail" in stages:
                        hidden(f - 1, CH - 1)
                    if j >= 1 and "ffn" in stages:
                        hidden(f, j - 1)
                    if j == 0 and "conv" in stages:
                        after(dve, s_h_hi, 1, c, 1)
                        v.tensor_tensor(h_stack[RED:2 * RED, :], h_full[RED:2 * RED, :],
                                        h_stack[RED:2 * RED, :].bitcast(F32), ALU.subtract).then_inc(s_h_lo, 1)
                    if "ln2" in stages:
                        if j == 3:
                            sum_x1(1)
                        if j == 6:
                            ln("ln2", 1, "x1_t", LN_T_EPS)
                        if j == 9:
                            ln("ln2", 3, "x1_t", LN_T_EPS)
                        if j == 14:
                            router_step(0)
                        if j >= 18:
                            router_step(2 + 2 * (j - 18))
                    if "ln1" in stages:
                        if j == 3:
                            ln("ln1", 1, "x_t", LN_C_EPS)
                        if j == 7:
                            ln("ln1", 3, "x_t", LN_C_EPS)
                    if "conv" in stages:
                        for u in UNITS_AT[j]:
                            unit(u)
                    if "ln2" in stages:
                        if j == 1:
                            sum_x1(0)
                        if j == 3:
                            sum_x1(2)
                        if j == 5:
                            ln("ln2", 0, "x1_t", LN_T_EPS)
                        if j == 6:
                            ln("ln2", 2, "x1_t", LN_T_EPS)
                        if j == 14:
                            router_step(1)
                        if j >= 18:
                            router_step(3 + 2 * (j - 18))
                    if "ln1" in stages:
                        if j == 2:
                            ln("ln1", 0, "x_t", LN_C_EPS)
                        if j == 4:
                            ln("ln1", 2, "x_t", LN_C_EPS)
                    if "conv" in stages:
                        for u in UNITS_AT[j - 1] if j else ():
                            if u in BY_VECTOR[1:]:
                                own_sum(u)
                    if j in (0, LAG) and "tail" in stages:
                        dve.wait_ge(s_bank_out, base)
                        gated(f - 1, EXPERTS - 2 + j // LAG)
                    if j > LAG and (j - LAG) % CPE == 0 and "ffn" in stages:
                        e = (j - LAG) // CPE - 1
                        dve.wait_ge(s_bank_out, bank_count(stages, base, f"gate{e}"))
                        gated(f, e)
                    if j == 9:
                        for i in w_pieces_in(t):
                            low_parts(i)
                    if j == 1 and "ffn" in stages:
                        dve.wait_ge(s_bank_out, bank_count(stages, base, "gates_t"))
                        v.tensor_tensor(gate_t[32:40, :], gate_f[32:40, :], gate_t[32:40, :].bitcast(F32),
                                        ALU.subtract).then_inc(s_gate_lo, 1)

            run(dve, body)

        @block.gpsimd
        def _(pool):
            g = nc.gpsimd
            g.memset(xn[:], 0.0).then_inc(s_setp, 1)
            g.memset(minus_half[:], -0.5)
            g.memset(euler[:], 2.718281828459045).then_inc(s_setp, 1)
            pool.wait_ge(s_setp, 2)
            pool.wait_ge(s_piece_lo, len(span_pieces))

            def body(t, stages, base):
                f, c, l = t, t + AHEAD["conv"], t + AHEAD["ln2"]

                def rsqrt(stage):
                    after(pool, s_ln[stage], 4, t + AHEAD[stage], 3)
                    after(pool, s_tok[stage], 1, t + AHEAD[stage], 0)
                    g.tensor_tensor(rstd[stage][:], veps[stage][:], minus_half[:], ALU.pow).then_inc(s_rstd[stage], 1)

                def unit(u):
                    if u in BY_POOL[1:]:
                        after(pool, s_prod, TAPS, c, u + 1)
                        k = BY_POOL.index(u)
                        if k == 1:
                            after(pool, s_accp, POOL_OPS, c, 0)
                            g.tensor_tensor(acc_p[:], prod[:, 0, :], prod[:, 1, :], ALU.add).then_inc(s_accp, 1)
                        else:
                            after(pool, s_accp, POOL_OPS, c, k - 1)
                            g.tensor_tensor(acc_p[:], acc_p[:], prod[:, k % PRING, :], ALU.add).then_inc(s_accp, 1)
                    elif u == TAPS - 1:
                        after(pool, s_prod, TAPS, c, TAPS)
                        after(pool, s_x_res, 16, c, 16)
                        after(pool, s_x1, 3, c - 1, 3)
                        g.tensor_tensor(single[:], x_res[:], prod[:, len(BY_POOL) % PRING, 0:N], ALU.add).then_inc(s_accp, 1)
                        after(pool, s_accp, POOL_OPS, c, POOL_OPS - 2)
                        g.tensor_tensor(x1_p[:], acc_p[:, 0:N], acc_p[:, N:2 * N], ALU.add).then_inc(s_accp, 1)

                def exponentials(q):
                    after(pool, s_rt, RT, l, 2)
                    g.tensor_tensor(lexp[:, q, :], euler[:, 0:EXPERTS], ldiff[:, q, :], ALU.pow).then_inc(s_exp, 1)

                def add_expert(tile, e):
                    after(pool, s_gy, EXPERTS, tile, e + 1)
                    after(pool, s_y, EXPERTS, tile, e)
                    if e == 0:
                        after(pool, s_x1_res, 1, tile, 1)
                        i = g.tensor_tensor(y_acc[:], x1_res[:], gy[:, 0, :], ALU.add)
                    elif e < EXPERTS - 1:
                        i = g.tensor_tensor(y_acc[:], y_acc[:], gy[:, e % 2, :], ALU.add)
                    else:
                        after(pool, s_out, 16, tile, 0)
                        i = g.tensor_tensor(y_out[:], y_acc[:], gy[:, e % 2, :], ALU.add)
                    i.then_inc(s_y, 1)

                for j in range(STEPS):
                    if j in (1, LAG + 1) and "tail" in stages:
                        add_expert(f - 1, EXPERTS - 2 + (j - 1) // LAG)
                    if j > LAG + 1 and (j - LAG - 1) % CPE == 0 and "ffn" in stages:
                        add_expert(f, (j - LAG - 1) // CPE - 1)
                    if j == 7 and "ln2" in stages:
                        rsqrt("ln2")
                    if j == 5 and "ln1" in stages:
                        rsqrt("ln1")
                    if j in (15, 16) and "ln2" in stages:
                        exponentials(2 * (j - 15))
                        exponentials(2 * (j - 15) + 1)
                    if "conv" in stages:
                        for u in UNITS_AT[j]:
                            unit(u)

            run(pool, body)


def kernel(x, L0_conv_reduce_w, L0_conv_reduce_b, L0_conv_span_w, L0_conv_span_b, L0_ffn_router_w,
           L0_ffn_w1, L0_ffn_w2, L0_ffn_w3):
    import numpy as np
    import concourse.bacc as bacc
    from concourse.bass_utils import run_bass_kernel_spmd

    f = np.float32
    x = np.asarray(x)
    xt = np.ascontiguousarray(x.reshape(B, C, H * W).transpose(1, 0, 2).reshape(C, B * H * W))
    w_red = np.ascontiguousarray(np.tile(np.asarray(L0_conv_reduce_w).T, (1, 3)))
    b_red = np.ascontiguousarray(np.tile(np.asarray(L0_conv_reduce_b), 3).reshape(3 * RED, 1))
    sw = np.asarray(L0_conv_span_w).reshape(GROUPS, KS * KS, RED)[:, TAP_ORDER, :]
    sw = np.repeat(sw.transpose(2, 1, 0), C // GROUPS, axis=2).reshape(RED, KS * KS * C)
    sbias = np.asarray(L0_conv_span_b).reshape(GROUPS, KS * KS)[:, TAP_ORDER]
    sbias = np.repeat(sbias.T, C // GROUPS, axis=1).reshape(1, KS * KS * C)
    w_span = np.ascontiguousarray(np.concatenate([sw, sw, sw, sbias, sbias], axis=0))

    def chunks(w):
        p = np.zeros((EXPERTS, CPE * HC, C), f)
        p[:, :HID] = w
        return p.reshape(CH, HC, C)

    w1 = np.ascontiguousarray(chunks(np.asarray(L0_ffn_w1)).reshape(CH * HC, C).T)
    w3 = np.ascontiguousarray(chunks(np.asarray(L0_ffn_w3)).reshape(CH * HC, C).T)
    w2 = np.ascontiguousarray(chunks(np.asarray(L0_ffn_w2).transpose(0, 2, 1)).transpose(1, 0, 2).reshape(HC, CH * C))
    select = np.zeros((40, EXPERTS, C), f)
    for e in range(EXPERTS):
        select[e, e] = 1.0
        select[32 + e, e] = 1.0
    arrays = {
        "x": xt, "w_red": w_red, "b_red": b_red, "w_span": w_span,
        "router": np.ascontiguousarray(np.asarray(L0_ffn_router_w).T), "w1": w1, "w3": w3, "w2": w2,
        "ident": np.eye(C, dtype=f), "select": select.reshape(40, EXPERTS * C),
        "iota": np.ascontiguousarray(np.broadcast_to(np.tile(np.arange(EXPERTS, dtype=f), SUBS), (SUB, SUBS * EXPERTS))),
    }
    nc = bacc.Bacc("TRN2", target_bir_lowering=False, num_devices=1)
    args = [nc.dram_tensor(f"in_{n}", a.shape, mybir.dt.from_np(a.dtype), kind="ExternalInput").ap() for n, a in arrays.items()]
    out = nc.dram_tensor("out", (C, B * H * W), F32, kind="ExternalOutput").ap()
    build(nc, *args, out)
    r = run_bass_kernel_spmd(nc, [{f"in_{n}": a for n, a in arrays.items()}], core_ids=[0])
    got = r.results[0]["out"]
    return np.ascontiguousarray(got.reshape(C, B, H * W).transpose(1, 0, 2).reshape(B, C, H, W))
```

```python
from contextlib import ExitStack

import concourse.bass as bass
from concourse import mybir

F32 = mybir.dt.float32
F32R = mybir.dt.float32r
U32 = mybir.dt.uint32
ALU = mybir.AluOpType
ACT = mybir.ActivationFunctionType
AX = mybir.AxisListType.X

B, C, H, W = 4, 128, 56, 56
GROUPS, KS, PAD, RED = 16, 7, 3, 32
EXPERTS, HID = 8, 341
LN_C_EPS, LN_T_EPS, GATE_EPS = 1e-6, 1e-5, 1e-9

ROWS = 8
N = ROWS * W
SUBS, SUB = 4, N // 4
PER_IMG = H // ROWS
TILES = B * PER_IMG
PW = W + 2 * PAD
IMG = (H + 2 * PAD) * PW

CPE = 3
HC = -(-HID // CPE)
CH = EXPERTS * CPE

PAIRS = [(dy * PW + dx, 1) for dy in range(KS) for dx in (0, 2, 4)] + [(dy * PW + 6, PW) for dy in (0, 2, 4)]
SINGLE = 6 * PW + 6
TAPS = len(PAIRS) + 1
BELOW = next(u for u, (tap, _) in enumerate(PAIRS) if tap // PW > PAD)
TAP_ORDER = [(dy * KS + dx + i) for dy in range(KS) for dx in (0, 2, 4) for i in (0, 1)] + [
    (dy + i) * KS + 6 for dy in (0, 2, 4) for i in (0, 1)] + [KS * KS - 1]

BY_VECTOR = (3, 6, 9, 13, 15, 18)
BY_POOL = [u for u in range(TAPS - 1) if u not in BY_VECTOR]
V_SUMS = len(BY_VECTOR) - 1
PRING = 5
HR = 3
POOL_OPS = len(BY_POOL) - 1 + 3

GW = 72

STEPS = CH
UNITS_AT = {s: [] for s in range(STEPS)}
_u = 0
for _s in range(STEPS):
    for _ in range(2 if _s == 11 else 1):
        UNITS_AT[_s].append(_u)
        _u += 1
assert _u == TAPS
LAG = 3

BANK_AT = {s: [] for s in range(STEPS)}
for _s, _use in ((1, ("ln1", "x_t")), (2, ("ffn", "gates_t")), (4, ("ln2", "x1_t")), (10, ("ln1", "xn")),
                 (12, ("ln2", "xn2")), (13, ("ln2", "logits")), (21, ("reduce", "h"))):
    BANK_AT[_s].append(_use)

AHEAD = {"ln1": 3, "reduce": 3, "conv": 2, "ln2": 1, "ffn": 0, "tail": -1}


def bodies():
    out = []
    for t in range(-AHEAD["ln1"], TILES + 1):
        stages = tuple(s for s, a in AHEAD.items() if 0 <= t + a < TILES)
        first = any(t + a == 0 for a in AHEAD.values())
        if out and out[-1][2] == stages and not out[-1][3] and not first:
            out[-1][1] = t + 1
        else:
            out.append([t, t + 1, stages, first])
    return [(a, b, s) for a, b, s, _ in out]


def bank_uses(stages):
    return [name for s in range(STEPS) for stage, name in BANK_AT[s] if stage in stages]


def build(nc, x, w_red, b_red, w_span, router, w1, w3, w2, ident, iota, out):
    with ExitStack() as ctx:
        def sb(name, shape, dt=F32):
            return ctx.enter_context(nc.sbuf_tensor(name, shape, dt))

        def psum(name, shape):
            return ctx.enter_context(nc.psum_tensor(name, shape, F32))

        def sem(name):
            return ctx.enter_context(nc.semaphore(name))

        kern_ps = psum("kern_ps", [C, 2, 2, 512])
        h1_ps = psum("h1_ps", [C, 512])
        h3_ps = psum("h3_ps", [C, 512])
        y_ps = psum("y_ps", [C, 512])
        bank = psum("bank", [C, 512])

        w1_hi, w1_lo = sb("w1_hi", [C, CH * HC], F32R), sb("w1_lo", [C, CH * HC], F32R)
        w3_hi, w3_lo = sb("w3_hi", [C, CH * HC], F32R), sb("w3_lo", [C, CH * HC], F32R)
        w2_sb = sb("w2_sb", [HC, CH, C])
        span = sb("span", [98, KS * KS * C], F32R)
        red_sb = sb("red_sb", [C, 3 * RED])
        bred_sb = sb("bred_sb", [3 * RED, 1])
        router_sb = sb("router_sb", [C, EXPERTS])
        ident_sb = sb("ident_sb", [C, C])
        iota_sb = sb("iota_sb", [SUB, SUBS, EXPERTS])
        minus_half = sb("minus_half", [SUB, SUBS])
        euler = sb("euler", [SUB, SUBS * EXPERTS])

        xn = sb("xn", [C, 2 * IMG])
        x_ln = sb("x_ln", [C, N])
        x_res = sb("x_res", [C, N])
        h_stack = sb("h_stack", [98, N], F32R)
        h_full = sb("h_full", [3 * RED, N])
        prod = sb("prod", [C, PRING, 2 * N])
        prod_v = sb("prod_v", [C, 2 * N])
        acc_p = sb("acc_p", [C, 2 * N])
        acc_v = sb("acc_v", [C, 2 * N])
        single = sb("single", [C, N])

        tok = {k: sb(f"tok_{k}", [SUB, SUBS, C]) for k in ("ln1", "ln2")}
        stats = {k: sb(f"stats_{k}", [SUB, SUBS, 6]) for k in ("ln1", "ln2")}
        mv = {k: sb(f"mv_{k}", [SUB, SUBS, 2]) for k in ("ln1", "ln2")}
        veps = {k: sb(f"veps_{k}", [SUB, SUBS]) for k in ("ln1", "ln2")}
        rstd = {k: sb(f"rstd_{k}", [SUB, SUBS]) for k in ("ln1", "ln2")}
        shift = {k: sb(f"shift_{k}", [SUB, SUBS]) for k in ("ln1", "ln2")}
        logits = sb("logits", [SUB, SUBS, EXPERTS])
        lmax = sb("lmax", [SUB, SUBS])
        ldiff = sb("ldiff", [SUB, SUBS, EXPERTS])
        lexp = sb("lexp", [SUB, SUBS, EXPERTS])
        lsum = sb("lsum", [SUB, SUBS])
        rsum = sb("rsum", [SUB, SUBS])
        probs = sb("probs", [SUB, SUBS, EXPERTS])
        top = sb("top", [SUB, SUBS, EXPERTS])
        top_at = sb("top_at", [SUB, SUBS, EXPERTS], U32)
        top_atf = sb("top_atf", [SUB, SUBS, 2])
        gden = sb("gden", [SUB, SUBS])
        grec = sb("grec", [SUB, SUBS])
        gtop = sb("gtop", [SUB, SUBS, 2])
        hot = sb("hot", [SUB, SUBS, 2, EXPERTS])
        gates = sb("gates", [SUB, SUBS, GW])
        gate_t = sb("gate_t", [EXPERTS, N])

        nothing = sb("nothing", [1, 1])

        x1 = sb("x1", [C, N])
        x1_p = sb("x1_p", [C, N])
        x1_res = sb("x1_res", [C, N])
        xn2 = sb("xn2", [C, N])
        xf_hi, xf_lo = sb("xf_hi", [C, N], F32R), sb("xf_lo", [C, N], F32R)
        silu = sb("silu", [HC, HR, N])
        h3_sb = sb("h3_sb", [HC, HR, N])
        hid = sb("hid", [HC, HR, N])
        gate_b = sb("gate_b", [C, 2, N])
        y_sb = sb("y_sb", [C, 2, N])
        gy = sb("gy", [C, 2, N])
        y_acc = sb("y_acc", [C, N])
        y_out = sb("y_out", [C, N])

        s_const = sem("s_const")
        s_w2_in = sem("s_w2_in")
        s_stage = [sem(f"s_stage{i}") for i in range(PRING)]
        s_w_stage = [sem(f"s_w_stage{i}") for i in range(3)]
        s_piece_hi = sem("s_piece_hi")
        s_piece_lo = sem("s_piece_lo")
        s_set = sem("s_set")
        s_setp = sem("s_setp")
        s_bank = sem("s_bank")
        s_bank_out = sem("s_bank_out")
        s_x_ln = sem("s_x_ln")
        s_x_res = sem("s_x_res")
        s_ln = {k: sem(f"s_{k}_v") for k in ("ln1", "ln2")}
        s_rstd = {k: sem(f"s_{k}_rstd") for k in ("ln1", "ln2")}
        s_tok = {k: sem(f"s_{k}_tok") for k in ("ln1", "ln2")}
        s_h_lo = sem("s_h_lo")
        s_kern = sem("s_kern")
        s_prod = sem("s_prod")
        s_accv = sem("s_accv")
        s_accp = sem("s_accp")
        s_x1 = sem("s_x1")
        s_x1_res = sem("s_x1_res")
        s_rt = sem("s_rt")
        s_exp = sem("s_exp")
        s_gate = [sem(f"s_gate{i}") for i in range(2)]
        s_xf_hi = sem("s_xf_hi")
        s_xf_lo = sem("s_xf_lo")
        s_h1 = sem("s_h1")
        s_silu = sem("s_silu")
        s_h3 = sem("s_h3")
        s_h3_out = sem("s_h3_out")
        s_h_hi = sem("s_h_hi")
        s_hid = sem("s_hid")
        s_w2 = sem("s_w2")
        s_y_out = sem("s_y_out")
        s_gy = sem("s_gy")
        s_y = sem("s_y")
        s_out = sem("s_out")

        RT = 14
        NCONST = 5

        span_pieces = [("span", i) for i in range(KS)]
        w_pieces = [(w, i) for w in ("w1", "w3") for i in range(4)]
        WCOLS = CH * HC // 4
        SCOLS = KS * C
        FIRST = -AHEAD["ln1"]

        def piece(i):
            if i < len(span_pieces):
                cols = slice(i * SCOLS, (i + 1) * SCOLS)
                return w_span[:, cols], prod[0:98, i % PRING, 0:SCOLS], s_stage[i % PRING], i // PRING, span[:, cols], None
            n = i - len(span_pieces)
            kind, k = w_pieces[n]
            cols = slice(k * WCOLS, (k + 1) * WCOLS)
            slot = (gate_b, gy, y_sb)[n % 3][:].rearrange("p a b -> p (a b)")[:, 0:WCOLS]
            src, hi, lo = (w1, w1_hi, w1_lo) if kind == "w1" else (w3, w3_hi, w3_lo)
            return src[:, cols], slot, s_w_stage[n % 3], n // 3, hi[:, cols], lo[:, cols]

        def pieces_at(t, j):
            if not isinstance(t, int) or t >= 0:
                return range(0)
            if t == FIRST and j < len(span_pieces):
                return range(j, j + 1)
            if j == 11:
                n = len(span_pieces) + 3 * (t - FIRST)
                return range(n, min(n + 3, len(span_pieces) + len(w_pieces)))
            return range(0)

        def after(eng, s, per, tile, k):
            v = tile * per + k
            if not isinstance(v, int) or v > 0:
                eng.wait_ge(s, v)

        def after_apart(s, per, tile, k):
            after(nc.vector, s, per, tile, k)
            nc.vector.memset(nothing[:], 0.0)

        def run(eng, body):
            base = 0
            for first, end, stages in bodies():
                uses = len(bank_uses(stages))
                if end - first == 1:
                    body(first, stages, base)
                else:
                    with eng.Fori(first, end) as t:
                        body(t, stages, (t - first) * uses + base)
                base += uses * (end - first)

        def bank_count(stages, base, name):
            return base + bank_uses(stages).index(name) + 1

        def xn_at(tile):
            return ((tile // PER_IMG) % 2) * IMG + (tile % PER_IMG) * (ROWS * PW)

        def window(start, pair_step=None):
            pdim = list(xn[:, 0:1].ap[0])
            dims = ([[pair_step, 2]] if pair_step else []) + [[PW, ROWS], [1, W]]
            return bass.AP(tensor=xn[:, 0:1].tensor, offset=start, ap=[pdim] + dims)

        def rows(ap):
            return ap.rearrange("p (r w) -> p r w", w=W)

        def pair_rows(ap):
            return ap.rearrange("p (i r w) -> p i r w", i=2, w=W)

        block = ctx.enter_context(nc.Block())

        @block.sync
        def _(sp):
            sp.dma_start(x_ln[:], x[:, 0:N]).then_inc(s_x_ln, 16)
            for dst, src in ((ident_sb[:], ident), (red_sb[:], w_red), (bred_sb[:], b_red), (router_sb[:], router),
                             (iota_sb[:].rearrange("p a b -> p (a b)"), iota)):
                sp.dma_start(dst, src).then_inc(s_const, 16)

            def load_piece(i):
                src, slot, arrived, _, _, _ = piece(i)
                slots, first = (PRING, 0) if i < len(span_pieces) else (3, len(span_pieces))
                if i - first >= slots:
                    sp.wait_ge(s_piece_lo, i - slots + 1)
                sp.dma_start(slot, src).then_inc(arrived, 16)

            for i in range(len(span_pieces)):
                load_piece(i)

            def load_gate(f, stages, base, e):
                if e == 0:
                    sp.wait_ge(s_bank_out, bank_count(stages, base, "gates_t"))
                else:
                    after(sp, s_gy, EXPERTS, f, e - 1)
                row = gate_t[e:e + 1, :]
                src = bass.AP(tensor=row.tensor, offset=row.offset, ap=[[row.ap[0][0], 1], [0, C], [1, N]])
                sp.dma_start(gate_b[:, e % 2, :], src).then_inc(s_gate[e % 2], 16)

            def body(t, stages, base):
                if "ln1" in stages and not (isinstance(t, int) and t == FIRST):
                    after(sp, s_tok["ln1"], 1, t + AHEAD["ln1"], 0)
                    sp.dma_start(x_ln[:], x[:, bass.ds((t + AHEAD["ln1"]) * N, N)]).then_inc(s_x_ln, 16)
                for i in pieces_at(t, 11):
                    load_piece(i)
                if isinstance(t, int) and t == -1:
                    sp.dma_start(w2_sb[:].rearrange("p a b -> p (a b)"), w2).then_inc(s_w2_in, 16)
                if "conv" in stages:
                    after(sp, s_accp, POOL_OPS, t + AHEAD["conv"], 0)
                    sp.dma_start(x_res[:], x[:, bass.ds((t + AHEAD["conv"]) * N, N)]).then_inc(s_x_res, 16)
                if "ffn" in stages:
                    load_gate(t, stages, base, 0)
                    load_gate(t, stages, base, 1)
                if "tail" in stages:
                    after(sp, s_y, EXPERTS, t - 1, EXPERTS)
                    sp.dma_start(out[:, bass.ds((t - 1) * N, N)], y_out[:]).then_inc(s_out, 16)
                if "ffn" in stages:
                    for e in range(2, EXPERTS):
                        load_gate(t, stages, base, e)

            run(sp, body)
            sp.wait_ge(s_out, 16 * TILES)

        @block.tensor
        def _(pe):
            mm = nc.tensor.matmul

            def body(t, stages, base):
                f, c = t, t + AHEAD["conv"]
                used = [0]

                def take_bank():
                    v = base + used[0]
                    if not isinstance(v, int) or v > 0:
                        pe.wait_ge(s_bank_out, v)
                    used[0] += 1

                def bank_use(stage, name):
                    take_bank()
                    if name == "h":
                        i = mm(bank[0:3 * RED, 0:N], red_sb[:], window(xn_at(t + AHEAD["reduce"]) + PAD * PW + PAD), start=True, stop=True)
                    elif name in ("x_t", "x1_t"):
                        if name == "x_t":
                            after(pe, s_x_ln, 16, t + AHEAD["ln1"], 16)
                        else:
                            after(pe, s_x1, 2, t + AHEAD["ln2"], 2)
                        src = x_ln if name == "x_t" else x1
                        for k in range(SUBS):
                            i = nc.tensor.transpose(bank[0:SUB, k * C:(k + 1) * C], src[:, k * SUB:(k + 1) * SUB], ident_sb[:])
                    elif name in ("xn", "xn2"):
                        after(pe, s_tok[stage], 1, t + AHEAD[stage], 1)
                        for k in range(SUBS):
                            i = nc.tensor.transpose(bank[:, k * SUB:(k + 1) * SUB], tok[stage][:, k, :], ident_sb[0:SUB, 0:SUB])
                    elif name == "logits":
                        for k in range(SUBS):
                            i = mm(bank[0:SUB, k * EXPERTS:(k + 1) * EXPERTS], xn2[:, k * SUB:(k + 1) * SUB], router_sb[:],
                                   start=True, stop=True)
                    elif name == "gates_t":
                        after(pe, s_rt, RT, f, RT)
                        for k in range(SUBS):
                            i = nc.tensor.transpose(bank[0:GW, k * SUB:(k + 1) * SUB], gates[:, k, :], ident_sb[0:SUB, 0:SUB])
                    i.then_inc(s_bank, 1)

                def unit(u):
                    if u == 0:
                        after(pe, s_h_lo, 1, c, 1)
                        after(pe, s_prod, TAPS, c, 0)
                    elif u >= 2:
                        after(pe, s_prod, TAPS, c, u - 1)
                    for i in range(2 if u < TAPS - 1 else 1):
                        k = 2 * u + i
                        last = mm(kern_ps[:, u % 2, i, 0:N], span[:, k * C:(k + 1) * C], h_stack[:], start=True, stop=True)
                    last.then_inc(s_kern, 1)

                def hidden(j, ps, hi, lo, done):
                    a, b = j * HC, (j + 1) * HC
                    if j == 0:
                        after(pe, s_xf_hi, 1, f, 1)
                    mm(ps[0:HC, 0:N], lo[:, a:b], xf_hi[:], start=True, stop=False)
                    mm(ps[0:HC, 0:N], hi[:, a:b], xf_hi[:], start=False, stop=False)
                    if j == 0:
                        after(pe, s_xf_lo, 1, f, 1)
                    mm(ps[0:HC, 0:N], hi[:, a:b], xf_lo[:], start=False, stop=True).then_inc(done, 1)

                def down(tile, j):
                    after(pe, s_hid, CH, tile, j + 1)
                    if j % CPE == 0:
                        after(pe, s_y_out, EXPERTS, tile, j // CPE)
                    mm(y_ps[:, 0:N], w2_sb[:, j, :], hid[:, j % HR, :], start=j % CPE == 0,
                       stop=j % CPE == CPE - 1).then_inc(s_w2, 1)

                if isinstance(t, int) and t == -AHEAD["conv"]:
                    pe.wait_ge(s_piece_lo, len(span_pieces))
                if isinstance(t, int) and t == 0:
                    pe.wait_ge(s_piece_lo, len(span_pieces) + len(w_pieces))
                    pe.wait_ge(s_w2_in, 16)
                for j in range(STEPS):
                    at_end = j in (0, STEPS - 1)
                    if j == 0 and "tail" in stages:
                        down(f - 1, CH - 3)
                        down(f - 1, CH - 2)
                    if j == 2 and "tail" in stages:
                        down(f - 1, CH - 1)
                    if j == STEPS - 1 and "ffn" in stages:
                        down(f, j - LAG)
                    if "ffn" in stages:
                        after(pe, s_silu, CH, f, j)
                        hidden(j, h1_ps, w1_hi, w1_lo, s_h1)
                        if at_end:
                            after(pe, s_h3_out, CH, f, j)
                            hidden(j, h3_ps, w3_hi, w3_lo, s_h3)
                    if "conv" in stages:
                        for u in UNITS_AT[j]:
                            unit(u)
                    if "ffn" in stages and not at_end:
                        if j >= LAG:
                            down(f, j - LAG)
                        after(pe, s_h3_out, CH, f, j)
                        hidden(j, h3_ps, w3_hi, w3_lo, s_h3)
                    for stage, name in BANK_AT[j]:
                        if stage in stages:
                            bank_use(stage, name)

            pe.wait_ge(s_const, 16 * NCONST)
            pe.wait_ge(s_set, 2)
            pe.wait_ge(s_setp, 2)
            run(pe, body)

        @block.scalar
        def _(act):
            act_f = nc.scalar.activation

            def high_parts(i):
                _, slot, arrived, n, hi, _ = piece(i)
                act.wait_ge(arrived, 16 * (n + 1))
                act_f(hi, slot, ACT.Copy).then_inc(s_piece_hi, 1)

            act.wait_ge(s_const, 16 * NCONST)
            act.wait_ge(s_setp, 2)

            def body(t, stages, base):
                f, c = t, t + AHEAD["conv"]
                used = [0]

                def bank_use(stage, name):
                    used[0] += 1
                    act.wait_ge(s_bank, base + used[0])
                    if name == "h":
                        after(act, s_h_lo, 1, t + AHEAD["reduce"], 0)
                        i = act_f(h_full[:], bank[0:3 * RED, 0:N], ACT.Identity, bias=bred_sb[:, 0:1])
                    elif name in ("x_t", "x1_t"):
                        i = act_f(tok[stage][:], bank[0:SUB, :].rearrange("p (a b) -> p a b", a=SUBS), ACT.Copy)
                    elif name == "xn":
                        dst = window(xn_at(t + AHEAD["ln1"]) + PAD * PW + PAD)
                        i = act_f(dst, rows(bank[:, 0:N]), ACT.Copy)
                    elif name == "xn2":
                        after(act, s_xf_lo, 1, t + AHEAD["ln2"], 0)
                        i = act_f(xn2[:], bank[:, 0:N], ACT.Copy)
                    elif name == "logits":
                        i = act_f(logits[:], bank[0:SUB, 0:SUBS * EXPERTS].rearrange("p (a b) -> p a b", a=SUBS), ACT.Copy)
                    elif name == "gates_t":
                        for slot in s_gate:
                            after(act, slot, 16 * EXPERTS // 2, f, 0)
                        after(act, s_gy, EXPERTS, f, -1)
                        i = act_f(gate_t[:], bank[0:EXPERTS, 0:N], ACT.Copy)
                    i.then_inc(s_bank_out, 1)

                def copy_y(tile, e):
                    after(act, s_w2, CH, tile, CPE * (e + 1))
                    after(act, s_gy, EXPERTS, tile, e - 1)
                    act_f(y_sb[:, e % 2, :], y_ps[:, 0:N], ACT.Copy).then_inc(s_y_out, 1)

                def normalise(stage, tile, half):
                    after(act, s_ln[stage], 4, tile, 4)
                    for k in (2 * half, 2 * half + 1):
                        i = act_f(tok[stage][:, k, :], tok[stage][:, k, :], ACT.Identity,
                                  bias=shift[stage][:, k:k + 1], scale=rstd[stage][:, k:k + 1])
                    if half:
                        i.then_inc(s_tok[stage], 1)

                for j in range(STEPS):
                    if j == 0 and "ffn" in stages:
                        after(act, s_h3, CH, f, 0)
                        act_f(xf_hi[:], xn2[:], ACT.Copy).then_inc(s_xf_hi, 1)
                    if j == 0 and "conv" in stages:
                        after(act, s_kern, TAPS, c, 0)
                        act.wait_ge(s_bank_out, base)
                        act_f(h_stack[0:3 * RED, :], h_full[:], ACT.Copy).then_inc(s_h_hi, 1)
                    if j == STEPS - 1 and "ffn" in stages:
                        copy_y(f, EXPERTS - 2)
                    if "ffn" in stages:
                        after(act, s_h1, CH, f, j + 1)
                        after(act, s_hid, CH, f, j + 1 - HR)
                        act_f(silu[:, j % HR, :], h1_ps[0:HC, 0:N], ACT.Silu).then_inc(s_silu, 1)
                    if j == LAG - 1 and "tail" in stages:
                        copy_y(f - 1, EXPERTS - 1)
                    if LAG <= j < STEPS - 1 and (j - LAG) % CPE == CPE - 1 and "ffn" in stages:
                        copy_y(f, (j - LAG) // CPE)
                    if "ffn" in stages:
                        after(act, s_h3, CH, f, j + 1)
                        act_f(h3_sb[:, j % HR, :], h3_ps[0:HC, 0:N], ACT.Copy).then_inc(s_h3_out, 1)
                    for stage, name in BANK_AT[j]:
                        if stage in stages:
                            bank_use(stage, name)
                    for i in pieces_at(t, j):
                        high_parts(i)
                    if j in (10, 11) and "ln2" in stages:
                        normalise("ln2", t + AHEAD["ln2"], j - 10)
                    if j in (8, 9) and "ln1" in stages:
                        normalise("ln1", t + AHEAD["ln1"], j - 8)
                    if j == 19 and "ln2" in stages:
                        after(act, s_y, EXPERTS, t, 1)
                        act_f(x1_res[:], x1[:], ACT.Copy).then_inc(s_x1_res, 1)

            run(act, body)

        @block.vector
        def _(dve):
            v = nc.vector
            v.memset(h_stack[96:98, :].bitcast(F32), 1.0).then_inc(s_set, 1)
            v.memset(gates[:], 0.0).then_inc(s_set, 1)

            def low_parts(i):
                _, slot, arrived, n, hi, lo = piece(i)
                dve.wait_ge(arrived, 16 * (n + 1))
                dve.wait_ge(s_piece_hi, i + 1)
                if lo is None:
                    hi, slot = hi[64:97, :], slot[64:97, :]
                    lo = hi
                v.tensor_tensor(lo, slot, hi.bitcast(F32), ALU.subtract).then_inc(s_piece_lo, 1)

            dve.wait_ge(s_const, 16 * NCONST)
            dve.wait_ge(s_set, 2)
            dve.wait_ge(s_setp, 2)

            def body(t, stages, base):
                f, c, l = t, t + AHEAD["conv"], t + AHEAD["ln2"]

                def ln(stage, k, name, eps):
                    tile = t + AHEAD[stage]
                    if k == 0:
                        dve.wait_ge(s_bank_out, bank_count(stages, base, name))
                        for q in range(SUBS):
                            i = v.bn_stats(stats[stage][:, q, :], tok[stage][:, q, :])
                    elif k == 1:
                        after_apart(s_ln[stage], 4, tile, 1)
                        for q in range(SUBS):
                            i = v.bn_aggr(mv[stage][:, q, :], stats[stage][:, q, :])
                    elif k == 2:
                        after(dve, s_ln[stage], 4, tile, 2)
                        i = v.tensor_scalar(veps[stage][:], mv[stage][:, :, 1], eps, None, ALU.add)
                    else:
                        after(dve, s_rstd[stage], 1, tile, 1)
                        i = v.scalar_tensor_tensor(out=shift[stage][:], in0=mv[stage][:, :, 0], scalar=-1.0,
                                                   in1=rstd[stage][:], op0=ALU.mult, op1=ALU.mult)
                    i.then_inc(s_ln[stage], 1)

                EACH = [SUB, SUBS, 2, EXPERTS]

                def router_step(k):
                    if k == 0:
                        dve.wait_ge(s_bank_out, bank_count(stages, base, "logits"))
                        i = v.tensor_reduce(lmax[:], logits[:], AX, ALU.max)
                    elif k == 2:
                        after(dve, s_exp, SUBS, l, SUBS)
                        i = v.tensor_reduce(lsum[:], lexp[:], AX, ALU.add)
                    else:
                        if k in (5, 6):
                            after_apart(s_rt, RT, l, k)
                        else:
                            after(dve, s_rt, RT, l, k)
                    if k == 1:
                        i = v.tensor_tensor(ldiff[:], logits[:], lmax[:].unsqueeze(2).broadcast_to([SUB, SUBS, EXPERTS]), ALU.subtract)
                    elif k == 3:
                        i = v.reciprocal(rsum[:], lsum[:])
                    elif k == 4:
                        i = v.tensor_tensor(probs[:], lexp[:], rsum[:].unsqueeze(2).broadcast_to([SUB, SUBS, EXPERTS]), ALU.mult)
                    elif k == 5:
                        for q in range(SUBS):
                            i = v.max(top[:, q, :], probs[:, q, :])
                    elif k == 6:
                        for q in range(SUBS):
                            i = v.max_index(top_at[:, q, :], top[:, q, :], probs[:, q, :])
                    elif k == 7:
                        i = v.tensor_copy(top_atf[:], top_at[:, :, 0:2])
                    elif k == 8:
                        i = v.scalar_tensor_tensor(out=gden[:], in0=top[:, :, 0], scalar=GATE_EPS, in1=top[:, :, 1],
                                                   op0=ALU.add, op1=ALU.add)
                    elif k == 9:
                        i = v.reciprocal(grec[:], gden[:])
                    elif k == 10:
                        i = v.tensor_tensor(gtop[:], top[:, :, 0:2], grec[:].unsqueeze(2).broadcast_to([SUB, SUBS, 2]), ALU.mult)
                    elif k == 11:
                        i = v.tensor_tensor(hot[:], iota_sb[:].unsqueeze(2).broadcast_to(EACH),
                                            top_atf[:].unsqueeze(3).broadcast_to(EACH), ALU.is_equal)
                    elif k == 12:
                        i = v.tensor_tensor(hot[:], hot[:], gtop[:].unsqueeze(3).broadcast_to(EACH), ALU.mult)
                    elif k == 13:
                        i = v.tensor_tensor(gates[:, :, 0:EXPERTS], hot[:, :, 0, :], hot[:, :, 1, :], ALU.add)
                    i.then_inc(s_rt, 1)

                def unit(u):
                    after(dve, s_kern, TAPS, c, u + 1)
                    if u == BELOW and "ln1" in stages:
                        dve.wait_ge(s_bank_out, bank_count(stages, base, "xn"))
                    start = xn_at(c)
                    if u in BY_VECTOR:
                        k = BY_VECTOR.index(u)
                        dst = prod_v if k else acc_v
                        if k:
                            after(dve, s_accv, V_SUMS, c, k - 1)
                        else:
                            after(dve, s_x1, 2, c - 1, 1)
                        dst = dst[:]
                    else:
                        k = BY_POOL.index(u) if u < TAPS - 1 else len(BY_POOL)
                        if k >= PRING:
                            after(dve, s_accp, POOL_OPS, c, max(k - PRING, 1))
                        else:
                            after(dve, s_accp, POOL_OPS, c - 1, max(i for i in range(len(BY_POOL) + 1) if i % PRING == k))
                        dst = prod[:, k % PRING, :]
                    if u == TAPS - 1:
                        v.tensor_tensor(rows(dst[:, 0:N]), rows(kern_ps[:, u % 2, 0, 0:N]),
                                        window(start + SINGLE), ALU.mult).then_inc(s_prod, 1)
                        return
                    v.tensor_tensor(pair_rows(dst), kern_ps[:, u % 2, :, 0:N].rearrange("p i (r w) -> p i r w", w=W),
                                    window(start + PAIRS[u][0], PAIRS[u][1]), ALU.mult).then_inc(s_prod, 1)

                def own_sum(u):
                    after(dve, s_prod, TAPS, c, u + 1)
                    after(dve, s_accv, V_SUMS, c, BY_VECTOR.index(u) - 1)
                    v.tensor_tensor(acc_v[:], acc_v[:], prod_v[:], ALU.add).then_inc(s_accv, 1)

                def sum_x1(k):
                    if k == 0:
                        after(dve, s_accv, V_SUMS, l, V_SUMS)
                        after(dve, s_x1_res, 1, l, 0)
                        i = v.tensor_tensor(x1[:], acc_v[:, 0:N], acc_v[:, N:2 * N], ALU.add)
                    else:
                        after(dve, s_accp, POOL_OPS, l, POOL_OPS)
                        after(dve, s_x1, 2, l, 1)
                        i = v.tensor_tensor(x1[:], x1[:], x1_p[:], ALU.add)
                    i.then_inc(s_x1, 1)

                def gated(tile, e):
                    after(dve, s_y_out, EXPERTS, tile, e + 1)
                    after(dve, s_gate[e % 2], 16 * EXPERTS // 2, tile, 16 * (e // 2 + 1))
                    after(dve, s_y, EXPERTS, tile, e - 1)
                    v.tensor_tensor(gy[:, e % 2, :], y_sb[:, e % 2, :], gate_b[:, e % 2, :], ALU.mult).then_inc(s_gy, 1)

                def hidden(tile, j):
                    after(dve, s_silu, CH, tile, j + 1)
                    after(dve, s_h3_out, CH, tile, j + 1)
                    after(dve, s_w2, CH, tile, j + 1 - HR)
                    v.tensor_tensor(hid[:, j % HR, :], silu[:, j % HR, :], h3_sb[:, j % HR, :], ALU.mult).then_inc(s_hid, 1)

                for j in range(STEPS):
                    if j == 0 and "ffn" in stages:
                        after(dve, s_xf_hi, 1, f, 1)
                        v.tensor_tensor(xf_lo[:], xn2[:], xf_hi[:].bitcast(F32), ALU.subtract).then_inc(s_xf_lo, 1)
                    if j == 0 and "conv" in stages:
                        after(dve, s_h_hi, 1, c, 1)
                        v.tensor_tensor(h_stack[RED:2 * RED, :], h_full[RED:2 * RED, :],
                                        h_stack[RED:2 * RED, :].bitcast(F32), ALU.subtract).then_inc(s_h_lo, 1)
                    if j == 0 and "tail" in stages:
                        hidden(f - 1, CH - 1)
                    if j >= 1 and "ffn" in stages:
                        hidden(f, j - 1)
                    if "ln2" in stages:
                        if j == 3:
                            sum_x1(1)
                        if j == 6:
                            ln("ln2", 1, "x1_t", LN_T_EPS)
                        if j == 9:
                            ln("ln2", 3, "x1_t", LN_T_EPS)
                        if j == 14:
                            router_step(0)
                        if j >= 18:
                            router_step(2 + 2 * (j - 18))
                    if "ln1" in stages:
                        if j == 3:
                            ln("ln1", 1, "x_t", LN_C_EPS)
                        if j == 7:
                            ln("ln1", 3, "x_t", LN_C_EPS)
                    if "conv" in stages:
                        for u in UNITS_AT[j]:
                            unit(u)
                    if "ln2" in stages:
                        if j == 1:
                            sum_x1(0)
                        if j == 5:
                            ln("ln2", 0, "x1_t", LN_T_EPS)
                        if j == 6:
                            ln("ln2", 2, "x1_t", LN_T_EPS)
                        if j == 14:
                            router_step(1)
                        if j >= 18:
                            router_step(3 + 2 * (j - 18))
                    if "ln1" in stages:
                        if j == 2:
                            ln("ln1", 0, "x_t", LN_C_EPS)
                        if j == 4:
                            ln("ln1", 2, "x_t", LN_C_EPS)
                    if "conv" in stages:
                        for u in UNITS_AT[j - 1] if j else ():
                            if u in BY_VECTOR[1:]:
                                own_sum(u)
                    if j in (0, LAG) and "tail" in stages:
                        gated(f - 1, EXPERTS - 2 + j // LAG)
                    if j > LAG and (j - LAG) % CPE == 0 and "ffn" in stages:
                        gated(f, (j - LAG) // CPE - 1)
                    for i in pieces_at(t, j):
                        low_parts(i)

            run(dve, body)

        @block.gpsimd
        def _(pool):
            g = nc.gpsimd
            g.memset(xn[:], 0.0).then_inc(s_setp, 1)
            g.memset(minus_half[:], -0.5)
            g.memset(euler[:], 2.718281828459045).then_inc(s_setp, 1)
            pool.wait_ge(s_setp, 2)

            def body(t, stages, base):
                f, c, l = t, t + AHEAD["conv"], t + AHEAD["ln2"]

                def rsqrt(stage):
                    after(pool, s_ln[stage], 4, t + AHEAD[stage], 3)
                    after(pool, s_tok[stage], 1, t + AHEAD[stage], 0)
                    g.tensor_tensor(rstd[stage][:], veps[stage][:], minus_half[:], ALU.pow).then_inc(s_rstd[stage], 1)

                def unit(u):
                    if u in BY_POOL[1:]:
                        after(pool, s_prod, TAPS, c, u + 1)
                        k = BY_POOL.index(u)
                        if k == 1:
                            after(pool, s_accp, POOL_OPS, c, 0)
                            g.tensor_tensor(acc_p[:], prod[:, 0, :], prod[:, 1, :], ALU.add).then_inc(s_accp, 1)
                        else:
                            after(pool, s_accp, POOL_OPS, c, k - 1)
                            g.tensor_tensor(acc_p[:], acc_p[:], prod[:, k % PRING, :], ALU.add).then_inc(s_accp, 1)
                    elif u == TAPS - 1:
                        after(pool, s_prod, TAPS, c, TAPS)
                        after(pool, s_x_res, 16, c, 16)
                        after(pool, s_x1, 2, c - 1, 2)
                        g.tensor_tensor(single[:], x_res[:], prod[:, len(BY_POOL) % PRING, 0:N], ALU.add).then_inc(s_accp, 1)
                        after(pool, s_accp, POOL_OPS, c, POOL_OPS - 3)
                        g.tensor_tensor(x1_p[:], acc_p[:, 0:N], acc_p[:, N:2 * N], ALU.add).then_inc(s_accp, 1)
                        after(pool, s_accp, POOL_OPS, c, POOL_OPS - 1)
                        g.tensor_tensor(x1_p[:], x1_p[:], single[:], ALU.add).then_inc(s_accp, 1)

                def exponentials(q):
                    after(pool, s_rt, RT, l, 2)
                    g.tensor_tensor(lexp[:, q, :], euler[:, 0:EXPERTS], ldiff[:, q, :], ALU.pow).then_inc(s_exp, 1)

                def add_expert(tile, e):
                    after(pool, s_gy, EXPERTS, tile, e + 1)
                    after(pool, s_y, EXPERTS, tile, e)
                    if e == 0:
                        after(pool, s_x1_res, 1, tile, 1)
                        i = g.tensor_tensor(y_acc[:], x1_res[:], gy[:, 0, :], ALU.add)
                    elif e < EXPERTS - 1:
                        i = g.tensor_tensor(y_acc[:], y_acc[:], gy[:, e % 2, :], ALU.add)
                    else:
                        after(pool, s_out, 16, tile, 0)
                        i = g.tensor_tensor(y_out[:], y_acc[:], gy[:, e % 2, :], ALU.add)
                    i.then_inc(s_y, 1)

                for j in range(STEPS):
                    if j in (1, LAG + 1) and "tail" in stages:
                        add_expert(f - 1, EXPERTS - 2 + (j - 1) // LAG)
                    if j > LAG + 1 and (j - LAG - 1) % CPE == 0 and "ffn" in stages:
                        add_expert(f, (j - LAG - 1) // CPE - 1)
                    if j == 7 and "ln2" in stages:
                        rsqrt("ln2")
                    if j == 5 and "ln1" in stages:
                        rsqrt("ln1")
                    if j in (14, 15) and "ln2" in stages:
                        exponentials(2 * (j - 14))
                        exponentials(2 * (j - 14) + 1)
                    if "conv" in stages:
                        for u in UNITS_AT[j]:
                            unit(u)

            run(pool, body)


def kernel(x, L0_conv_reduce_w, L0_conv_reduce_b, L0_conv_span_w, L0_conv_span_b, L0_ffn_router_w,
           L0_ffn_w1, L0_ffn_w2, L0_ffn_w3):
    import numpy as np
    import concourse.bacc as bacc
    from concourse.bass_utils import run_bass_kernel_spmd

    f = np.float32
    x = np.asarray(x)
    xt = np.ascontiguousarray(x.reshape(B, C, H * W).transpose(1, 0, 2).reshape(C, B * H * W))
    w_red = np.ascontiguousarray(np.tile(np.asarray(L0_conv_reduce_w).T, (1, 3)))
    b_red = np.ascontiguousarray(np.tile(np.asarray(L0_conv_reduce_b), 3).reshape(3 * RED, 1))
    sw = np.asarray(L0_conv_span_w).reshape(GROUPS, KS * KS, RED)[:, TAP_ORDER, :]
    sw = np.repeat(sw.transpose(2, 1, 0), C // GROUPS, axis=2).reshape(RED, KS * KS * C)
    sbias = np.asarray(L0_conv_span_b).reshape(GROUPS, KS * KS)[:, TAP_ORDER]
    sbias = np.repeat(sbias.T, C // GROUPS, axis=1).reshape(1, KS * KS * C)
    w_span = np.ascontiguousarray(np.concatenate([sw, sw, sw, sbias, sbias], axis=0))

    def chunks(w):
        p = np.zeros((EXPERTS, CPE * HC, C), f)
        p[:, :HID] = w
        return p.reshape(CH, HC, C)

    w1 = np.ascontiguousarray(chunks(np.asarray(L0_ffn_w1)).reshape(CH * HC, C).T)
    w3 = np.ascontiguousarray(chunks(np.asarray(L0_ffn_w3)).reshape(CH * HC, C).T)
    w2 = np.ascontiguousarray(chunks(np.asarray(L0_ffn_w2).transpose(0, 2, 1)).transpose(1, 0, 2).reshape(HC, CH * C))
    arrays = {
        "x": xt, "w_red": w_red, "b_red": b_red, "w_span": w_span,
        "router": np.ascontiguousarray(np.asarray(L0_ffn_router_w).T), "w1": w1, "w3": w3, "w2": w2,
        "ident": np.eye(C, dtype=f),
        "iota": np.ascontiguousarray(np.broadcast_to(np.tile(np.arange(EXPERTS, dtype=f), SUBS), (SUB, SUBS * EXPERTS))),
    }
    nc = bacc.Bacc("TRN2", target_bir_lowering=False, num_devices=1)
    args = [nc.dram_tensor(f"in_{n}", a.shape, mybir.dt.from_np(a.dtype), kind="ExternalInput").ap() for n, a in arrays.items()]
    out = nc.dram_tensor("out", (C, B * H * W), F32, kind="ExternalOutput").ap()
    build(nc, *args, out)
    r = run_bass_kernel_spmd(nc, [{f"in_{n}": a for n, a in arrays.items()}], core_ids=[0])
    got = r.results[0]["out"]
    return np.ascontiguousarray(got.reshape(C, B, H * W).transpose(1, 0, 2).reshape(B, C, H, W))
```
